# Optimizing a Trainium2 kernel written in Bass

```python
import numpy as np
import jax
import jax.numpy as jnp

def _softmax(x, axis=-1):
    return jax.nn.softmax(x, axis=axis)

def _gelu(x):
    return jax.nn.gelu(x, approximate=True)

def _silu(x):
    return jax.nn.silu(x)

def _sigmoid(x):
    return jax.nn.sigmoid(x)

def _layernorm(x, axis=-1, eps=1e-05):
    m = jnp.mean(x, axis=axis, keepdims=True)
    v = jnp.var(x, axis=axis, keepdims=True)
    return (x - m) / jnp.sqrt(v + eps)

def _scatter_add(tgt, idx, src, axis=0):
    return tgt.at[idx].add(src)

def _segment_sum(src, seg, n):
    return jax.ops.segment_sum(src, seg, n)
kernel_name = 'mk_perceiver_d1_seqx_r2_56416b'

def setup_inputs(seed: int=0):
    np.random.seed(seed)
    _w = jnp.asarray

    def _rec_inputs():
        import jax
        import jax.numpy as jnp
        _rk = jax.random.key(seed)
        x = 7.22e-05 + 1 * jax.random.normal(jax.random.fold_in(_rk, 1), (1, 512, 1024), jnp.float32)
        _lenS = 512 - jax.random.randint(jax.random.fold_in(_rk, 7), (1,), 0, max(1, 512 // 4) + 1, jnp.int32)
        _lenS2 = 8192 - jax.random.randint(jax.random.fold_in(_rk, 8), (1,), 0, max(1, 8192 // 4) + 1, jnp.int32)
        _ctx_1024P = jax.random.normal(jax.random.fold_in(_rk, 11), (1, 16, 512), jnp.float32)
        _ctx_1024c = jax.random.dirichlet(jax.random.fold_in(_rk, 511), 0.3 * jnp.ones((16,), jnp.float32), (1, 8192))
        _ctx_1024t = jnp.einsum('bsk,bkd->bsd', _ctx_1024c, _ctx_1024P)
        _ctx_1024t = _ctx_1024t * jax.lax.rsqrt(jnp.mean(jnp.square(_ctx_1024t)) + 1e-12) * 0.953939
        ctx_1024 = -0.000673644 + 1.00013 * (_ctx_1024t + 0.3 * jax.random.normal(jax.random.fold_in(_rk, 611), (1, 8192, 512), jnp.float32))
        return (x, ctx_1024)
    x, ctx_1024 = _rec_inputs()

    def _L0_xattn_setup():
        import jax, jax.numpy as jnp
        import numpy as np
        B, S1, S2, DCA = (2, 1024, 512, 16)
        QDIM, KDIM, H = (1024, 512, 16)
        HD = QDIM // H
        SCALE = HD ** (-0.5)
        EPS = 1e-06
        DCA_WEIGHT = 1.0

        def _ln(t, w, b):
            m = jnp.mean(t, axis=-1, keepdims=True)
            v = jnp.var(t, axis=-1, keepdims=True)
            return (t - m) * jax.lax.rsqrt(v + EPS) * w + b

        def _attn(q, k, v):
            s = jnp.einsum('bhqd,bhkd->bhqk', q, k) * SCALE
            p = jax.nn.softmax(s, axis=-1)
            return jnp.einsum('bhqk,bhkd->bhqd', p, v)
        key = jax.random.key(seed)
        ks = jax.random.split(key, 8)
        w = lambda k, shape: jax.random.normal(k, shape, jnp.float32) * 0.02
        return {'x': jax.random.normal(ks[0], (B, S1, QDIM), jnp.float32), 'y': jax.random.normal(ks[1], (B, S2 + DCA, KDIM), jnp.float32), 'Wq': w(ks[2], (QDIM, QDIM)), 'bq': jnp.zeros((QDIM,), jnp.float32), 'Wk': w(ks[3], (KDIM, QDIM)), 'bk': jnp.zeros((QDIM,), jnp.float32), 'Wv': w(ks[4], (KDIM, QDIM)), 'bv': jnp.zeros((QDIM,), jnp.float32), 'Wkv_dca': w(ks[5], (KDIM, 2 * QDIM)), 'bkv_dca': jnp.zeros((2 * QDIM,), jnp.float32), 'qn_w': jnp.ones((HD,), jnp.float32), 'qn_b': jnp.zeros((HD,), jnp.float32), 'kn_w': jnp.ones((HD,), jnp.float32), 'kn_b': jnp.zeros((HD,), jnp.float32), 'kn_dca_w': jnp.ones((HD,), jnp.float32), 'kn_dca_b': jnp.zeros((HD,), jnp.float32), 'Wo': w(ks[6], (QDIM, QDIM)), 'bo': jnp.zeros((QDIM,), jnp.float32)}
    _L0_xattn_all = _L0_xattn_setup()
    _L0_xattn_in = {k: v for k, v in _L0_xattn_all.items() if k in ('Wq', 'bq', 'Wk', 'bk', 'Wv', 'bv', 'Wkv_dca', 'bkv_dca', 'qn_w', 'qn_b', 'kn_w', 'kn_b', 'kn_dca_w', 'kn_dca_b', 'Wo', 'bo')}
    del _L0_xattn_all

    def _L0_attn_setup():
        import jax, jax.numpy as jnp
        import numpy as np
        B, L, D = (2, 1024, 1024)
        H, HK = (32, 8)
        HD = D // H
        W = 512
        key = jax.random.key(seed)
        ks = jax.random.split(key, 5)
        s = 1.0 / np.sqrt(D).astype(np.float32)
        return {'x': jax.random.normal(ks[0], (B, L, D), jnp.float32), 'wq': jax.random.normal(ks[1], (D, D), jnp.float32) * s, 'wk': jax.random.normal(ks[2], (D, HK * HD), jnp.float32) * s, 'wv': jax.random.normal(ks[3], (D, HK * HD), jnp.float32) * s, 'wo': jax.random.normal(ks[4], (D, D), jnp.float32) * s}
    _L0_attn_all = _L0_attn_setup()
    _L0_attn_in = {k: v for k, v in _L0_attn_all.items() if k in ('wq', 'wk', 'wv', 'wo')}
    del _L0_attn_all

    def _L0_ffn_setup():
        import jax, jax.numpy as jnp
        import numpy as np
        TOP_K = 4
        ROUTED_SCALE = 1.0
        NORM_TOPK = True
        B, S, H = (1, 1024, 1024)
        E, I = (16, 384)
        IS = 384
        key = jax.random.key(seed)
        ks = jax.random.split(key, 8)
        s = 0.02
        return {'hidden_states': jax.random.normal(ks[0], (B, S, H), jnp.float32), 'router_w': jax.random.normal(ks[1], (E, H), jnp.float32) * s, 'e_bias': jax.random.normal(ks[2], (E,), jnp.float32) * s, 'gate_up_proj': jax.random.normal(ks[3], (E, 2 * I, H), jnp.float32) * s, 'down_proj': jax.random.normal(ks[4], (E, H, I), jnp.float32) * s, 'shared_gate_w': jax.random.normal(ks[5], (IS, H), jnp.float32) * s, 'shared_up_w': jax.random.normal(ks[6], (IS, H), jnp.float32) * s, 'shared_down_w': jax.random.normal(ks[7], (H, IS), jnp.float32) * s}
    _L0_ffn_all = _L0_ffn_setup()
    _L0_ffn_in = {k: v for k, v in _L0_ffn_all.items() if k in ('router_w', 'e_bias', 'gate_up_proj', 'down_proj', 'shared_gate_w', 'shared_up_w', 'shared_down_w')}
    del _L0_ffn_all
    return {'x': x, 'ctx_1024': ctx_1024, 'L0_xattn_Wq': _L0_xattn_in['Wq'], 'L0_xattn_bq': _L0_xattn_in['bq'], 'L0_xattn_Wk': _L0_xattn_in['Wk'], 'L0_xattn_bk': _L0_xattn_in['bk'], 'L0_xattn_Wv': _L0_xattn_in['Wv'], 'L0_xattn_bv': _L0_xattn_in['bv'], 'L0_xattn_Wkv_dca': _L0_xattn_in['Wkv_dca'], 'L0_xattn_bkv_dca': _L0_xattn_in['bkv_dca'], 'L0_xattn_qn_w': _L0_xattn_in['qn_w'], 'L0_xattn_qn_b': _L0_xattn_in['qn_b'], 'L0_xattn_kn_w': _L0_xattn_in['kn_w'], 'L0_xattn_kn_b': _L0_xattn_in['kn_b'], 'L0_xattn_kn_dca_w': _L0_xattn_in['kn_dca_w'], 'L0_xattn_kn_dca_b': _L0_xattn_in['kn_dca_b'], 'L0_xattn_Wo': _L0_xattn_in['Wo'], 'L0_xattn_bo': _L0_xattn_in['bo'], 'L0_attn_wq': _L0_attn_in['wq'], 'L0_attn_wk': _L0_attn_in['wk'], 'L0_attn_wv': _L0_attn_in['wv'], 'L0_attn_wo': _L0_attn_in['wo'], 'L0_ffn_router_w': _L0_ffn_in['router_w'], 'L0_ffn_e_bias': _L0_ffn_in['e_bias'], 'L0_ffn_gate_up_proj': _L0_ffn_in['gate_up_proj'], 'L0_ffn_down_proj': _L0_ffn_in['down_proj'], 'L0_ffn_shared_gate_w': _L0_ffn_in['shared_gate_w'], 'L0_ffn_shared_up_w': _L0_ffn_in['shared_up_w'], 'L0_ffn_shared_down_w': _L0_ffn_in['shared_down_w']}

def reference(x, ctx_1024, L0_xattn_Wq, L0_xattn_bq, L0_xattn_Wk, L0_xattn_bk, L0_xattn_Wv, L0_xattn_bv, L0_xattn_Wkv_dca, L0_xattn_bkv_dca, L0_xattn_qn_w, L0_xattn_qn_b, L0_xattn_kn_w, L0_xattn_kn_b, L0_xattn_kn_dca_w, L0_xattn_kn_dca_b, L0_xattn_Wo, L0_xattn_bo, L0_attn_wq, L0_attn_wk, L0_attn_wv, L0_attn_wo, L0_ffn_router_w, L0_ffn_e_bias, L0_ffn_gate_up_proj, L0_ffn_down_proj, L0_ffn_shared_gate_w, L0_ffn_shared_up_w, L0_ffn_shared_down_w):
    import jax
    import jax.numpy as jnp

    def _L0_xattn_ref(x, y, Wq, bq, Wk, bk, Wv, bv, Wkv_dca, bkv_dca, qn_w, qn_b, kn_w, kn_b, kn_dca_w, kn_dca_b, Wo, bo):
        import jax, jax.numpy as jnp
        import numpy as np
        B, S1, S2, DCA = (2, 1024, 512, 16)
        QDIM, KDIM, H = (1024, 512, 16)
        HD = QDIM // H
        SCALE = HD ** (-0.5)
        EPS = 1e-06
        DCA_WEIGHT = 1.0

        def _ln(t, w, b):
            m = jnp.mean(t, axis=-1, keepdims=True)
            v = jnp.var(t, axis=-1, keepdims=True)
            return (t - m) * jax.lax.rsqrt(v + EPS) * w + b

        def _attn(q, k, v):
            s = jnp.einsum('bhqd,bhkd->bhqk', q, k) * SCALE
            p = jax.nn.softmax(s, axis=-1)
            return jnp.einsum('bhqk,bhkd->bhqd', p, v)
        b, s1, _ = x.shape
        y_dca = y[:, -DCA:, :]
        y_main = y[:, :-DCA, :]
        kv_dca = (y_dca @ Wkv_dca + bkv_dca).reshape(b, DCA, 2, H, HD)
        k_dca = _ln(kv_dca[:, :, 0], kn_dca_w, kn_dca_b)
        v_dca = kv_dca[:, :, 1]
        s2 = y_main.shape[1]
        q = _ln((x @ Wq + bq).reshape(b, s1, H, HD), qn_w, qn_b)
        kv = jnp.concatenate([y_main @ Wk + bk, y_main @ Wv + bv], axis=-1)
        kv = kv.reshape(b, s2, H, 2 * HD)
        k = _ln(kv[..., :HD], kn_w, kn_b)
        v = kv[..., HD:]
        qT = q.transpose(0, 2, 1, 3)
        ctx = _attn(qT, k.transpose(0, 2, 1, 3), v.transpose(0, 2, 1, 3))
        ctx = ctx.transpose(0, 2, 1, 3).reshape(b, s1, QDIM)
        ctx_dca = _attn(qT, k_dca.transpose(0, 2, 1, 3), v_dca.transpose(0, 2, 1, 3))
        ctx_dca = ctx_dca.transpose(0, 2, 1, 3).reshape(b, s1, QDIM)
        ctx = ctx + DCA_WEIGHT * ctx_dca
        return ctx @ Wo + bo

    def _L0_attn_ref(x, wq, wk, wv, wo):
        import jax, jax.numpy as jnp
        import numpy as np
        B, L, D = (2, 1024, 1024)
        H, HK = (32, 8)
        HD = D // H
        W = 512
        Bb, Ll, Dm = x.shape
        n_rep = H // HK
        q = (x @ wq).reshape(Bb, Ll, H, HD).transpose(0, 2, 1, 3)
        k = jnp.repeat((x @ wk).reshape(Bb, Ll, HK, HD), n_rep, axis=2).transpose(0, 2, 1, 3)
        v = jnp.repeat((x @ wv).reshape(Bb, Ll, HK, HD), n_rep, axis=2).transpose(0, 2, 1, 3)
        scores = jnp.einsum('bhqd,bhkd->bhqk', q, k) / jnp.float32(np.sqrt(HD))
        i = jnp.arange(Ll)[:, None]
        j = jnp.arange(Ll)[None, :]
        amask = jnp.where((j >= i - W) & (j < i), jnp.float32(-10000000000.0), jnp.float32(0.0))
        attn = jax.nn.softmax(scores + amask[None, None, :, :], axis=-1)
        out = jnp.einsum('bhqk,bhkd->bqhd', attn, v).reshape(Bb, Ll, Dm)
        return out @ wo

    def _L0_ffn_ref(hidden_states, router_w, e_bias, gate_up_proj, down_proj, shared_gate_w, shared_up_w, shared_down_w):
        import jax, jax.numpy as jnp
        import numpy as np
        TOP_K = 4
        ROUTED_SCALE = 1.0
        NORM_TOPK = True
        B, S, H = (1, 1024, 1024)
        E, I = (16, 384)
        IS = 384
        orig_shape = hidden_states.shape
        x = hidden_states.reshape(-1, orig_shape[-1])
        T = x.shape[0]
        scores = jax.nn.sigmoid(x @ router_w.T)
        _, topk_idx = jax.lax.top_k(scores + e_bias[None, :], TOP_K)
        topk_w = jnp.take_along_axis(scores, topk_idx, axis=1)
        if NORM_TOPK:
            topk_w = topk_w / (topk_w.sum(axis=-1, keepdims=True) + 1e-20)
        topk_w = topk_w * ROUTED_SCALE
        combine = jnp.zeros((T, E), x.dtype).at[jnp.arange(T)[:, None], topk_idx].add(topk_w)

        def step(acc, xs):
            gu_w, d_w, c = xs
            gu = x @ gu_w.T
            g, u = jnp.split(gu, 2, axis=1)
            y = jax.nn.silu(g) * u @ d_w.T
            return (acc + c[:, None] * y, None)
        routed, _ = jax.lax.scan(step, jnp.zeros_like(x), (gate_up_proj, down_proj, combine.T))
        shared = jax.nn.silu(x @ shared_gate_w.T) * (x @ shared_up_w.T) @ shared_down_w.T
        return (routed + shared).reshape(orig_shape)
    x = x + _L0_xattn_ref(_layernorm(x, axis=-1), ctx_1024, L0_xattn_Wq, L0_xattn_bq, L0_xattn_Wk, L0_xattn_bk, L0_xattn_Wv, L0_xattn_bv, L0_xattn_Wkv_dca, L0_xattn_bkv_dca, L0_xattn_qn_w, L0_xattn_qn_b, L0_xattn_kn_w, L0_xattn_kn_b, L0_xattn_kn_dca_w, L0_xattn_kn_dca_b, L0_xattn_Wo, L0_xattn_bo)
    x = x + _L0_attn_ref(_layernorm(x, axis=-1), L0_attn_wq, L0_attn_wk, L0_attn_wv, L0_attn_wo)
    x = x + _L0_ffn_ref(_layernorm(x, axis=-1), L0_ffn_router_w, L0_ffn_e_bias, L0_ffn_gate_up_proj, L0_ffn_down_proj, L0_ffn_shared_gate_w, L0_ffn_shared_up_w, L0_ffn_shared_down_w)
    return x

_drawn_inputs = setup_inputs


def setup_inputs(seed=0):
    import zlib

    import numpy as np

    out = dict(_drawn_inputs(seed))
    spreads = {'L0_xattn_bq': (0.0, 0.362),
     'L0_xattn_bk': (0.0, 0.1),
     'L0_xattn_bv': (0.0, 0.1),
     'L0_xattn_bkv_dca': (0.0, 0.1),
     'L0_xattn_qn_w': (1.0, 0.6),
     'L0_xattn_qn_b': (0.0, 0.68),
     'L0_xattn_kn_w': (1.0, 0.6),
     'L0_xattn_kn_b': (0.0, 0.8),
     'L0_xattn_kn_dca_w': (1.0, 0.6),
     'L0_xattn_kn_dca_b': (0.0, 0.8),
     'L0_xattn_bo': (0.0, 0.1)}
    factors = {'L0_ffn_e_bias': 4.38}
    for name, (base, spread) in spreads.items():
        noise = np.random.default_rng([zlib.crc32(name.encode()), seed]).standard_normal(out[name].shape)
        drawn = base * np.exp(spread * noise) if base else spread * noise
        out[name] = jnp.asarray(drawn.astype(out[name].dtype))
    for name, factor in factors.items():
        out[name] = (out[name] * factor).astype(out[name].dtype)
    return out
```

```python
from contextlib import ExitStack

import concourse.bass as bass
from concourse import mybir

F32 = mybir.dt.float32
F32R = mybir.dt.float32r
ALU = mybir.AluOpType
ACT = mybir.ActivationFunctionType
AX = mybir.AxisListType

P = 128
TOK = 512
TM = TOK // P
D = 1024
DK = D // P
CTX = 8192
DCA = 16
KC = 512
CK = KC // P
XH = 16
XD = D // XH
PAIRS = XH // 2
CHUNK = 512
STEPS = CTX // CHUNK
KT = CHUNK // P
XSCALE = float(XD) ** -0.5
RANGE = 60.0
NEG = -1.0e30


def broadcast_rows(vector, rows):
    return vector.rearrange("(o n) -> o n", o=1).broadcast_to([rows, vector.shape[0]])


def prepare(nc, io, keep):
    with ExitStack() as ctx:
        def sb(name, shape, dt=F32):
            return ctx.enter_context(nc.sbuf_tensor("p_" + name, shape, dt))

        def sem(name):
            return nc.alloc_semaphore("p_" + name)

        x_sb = sb("x_sb", [P, TM, D])
        xn = sb("xn", [P, TM, D])
        xt_hi = sb("xt_hi", [P, DK, TOK], F32R)
        xt_lo = sb("xt_lo", [P, DK, TOK], F32R)
        wq_raw = sb("wq_raw", [P, 2, D])
        wq_hi = sb("wq_hi", [P, DK, D], F32R)
        wq_lo = sb("wq_lo", [P, DK, D], F32R)
        bq_row = sb("bq_row", [P, D])
        qn_w = sb("qn_w", [P, XD])
        qn_b = sb("qn_b", [P, XD])
        kn_col = sb("kn_col", [P, 1])
        head_mean = sb("head_mean", [P, P])
        head_ones = sb("head_ones", [P, 2, P])
        small = sb("small", [P, 160])
        half_power = sb("half_power", [P, 2 * XH])
        stats = sb("stats", [P, TM, 2, 6])
        means = sb("means", [P, TM, 2])
        square = sb("square", [P, D])
        qk = sb("qk", [P, 2, TOK])
        q_hi = sb("q_hi", [P, 2, TOK], F32R)
        q_lo = sb("q_lo", [P, 2, TOK], F32R)
        bound = sb("bound", [P, XH])
        tail_mask = sb("tail_mask", [P, 1])
        bk_raw = sb("bk_raw", [P, PAIRS])
        xr = x_sb[:, 0:2, :]
        q = xn

        bank = [ctx.enter_context(nc.psum_tensor(f"p_bank{i}", [P, 512], F32)) for i in range(8)]

        in_x, in_w = sem("in_x"), sem("in_w")
        in_wq = [sem(f"in_wq{i}") for i in range(2)]
        consts, v_chain, pool_chain, a_chain = sem("consts"), sem("v_chain"), sem("pool_chain"), sem("a_chain")
        var_ready, rstd_ready = sem("var_ready"), sem("rstd_ready")
        xn_ready, xt_banked, xt_hi_ready, xt_lo_ready = sem("xn_ready"), sem("xt_banked"), sem("xt_hi_ready"), sem("xt_lo_ready")
        wq_hi_ready, wq_lo_ready = sem("wq_hi_ready"), sem("wq_lo_ready")
        q_banked, q_taken, q_ready = sem("q_banked"), sem("q_taken"), sem("q_ready")
        qt_banked, qk_ready, q_hi_ready, q_lo_ready = sem("qt_banked"), sem("qk_ready"), sem("q_hi_ready"), sem("q_lo_ready")
        q_stored = [sem(f"q_stored{i}") for i in range(2)]
        qt_copied = sem("qt_copied")
        sq_ready, norm_banked, norm_taken = sem("sq_ready"), sem("norm_banked"), sem("norm_taken")
        bmean_banked, bound_var, bound_ready = sem("bmean_banked"), sem("bound_var"), sem("bound_ready")

        with nc.Block() as block:
            def x_hi(act, k):
                act.wait_ge(xt_banked, k + 1)
                nc.scalar.activation(xt_hi[:, k, :], bank[k % 4][:], ACT.Copy).then_inc(xt_hi_ready, 1)

            def x_lo(dve, k):
                dve.wait_ge(xt_hi_ready, k + 1)
                nc.vector.tensor_tensor(xt_lo[:, k, :], bank[k % 4][:], xt_hi[:, k, :].bitcast(F32),
                                        ALU.subtract).then_inc(xt_lo_ready, 1)

            @block.sync
            def _(sp):
                for m in range(TM):
                    sp.dma_start(x_sb[:, m, :], io["x"][0, m * P:(m + 1) * P, :]).then_inc(in_x, 16)
                for k in range(DK):
                    if k >= 2:
                        sp.wait_ge(wq_hi_ready, k - 1)
                        sp.wait_ge(wq_lo_ready, k - 1)
                    sp.dma_start(wq_raw[:, k % 2, :], io["wq"][k * P:(k + 1) * P, :]).then_inc(in_wq[k % 2], 16)
                for p in range(PAIRS):
                    sp.wait_ge(q_hi_ready, p + 1)
                    sp.wait_ge(q_lo_ready, p + 1)
                    sp.dma_start(keep["q_dram"][p, :, 0, :].bitcast(F32), q_hi[:, p % 2, :].bitcast(F32)).then_inc(q_stored[p % 2], 16)
                    sp.dma_start(keep["q_dram"][p, :, 1, :].bitcast(F32), q_lo[:, p % 2, :].bitcast(F32)).then_inc(q_stored[p % 2], 16)
                p = PAIRS
                sp.dma_start(keep["q_dram"][PAIRS, :, 0, :].bitcast(F32), q_hi[:, (PAIRS - 1) % 2, :].bitcast(F32)).then_inc(q_stored[p % 2], 16)
                sp.dma_start(keep["q_dram"][PAIRS, :, 1, :].bitcast(F32), q_lo[:, (PAIRS - 1) % 2, :].bitcast(F32)).then_inc(q_stored[p % 2], 16)
                sp.wait_ge(q_stored[0], 32 * (PAIRS // 2 + 1))
                sp.wait_ge(q_stored[1], 32 * (PAIRS // 2))

            @block.gpsimd
            def _(pool):
                nc.gpsimd.memset(keep["identity"][:], 0.0).then_inc(pool_chain, 1)
                nc.gpsimd.memset(tail_mask[:], 0.0).then_inc(pool_chain, 1)
                nc.gpsimd.memset(half_power[:, 0:XH], -0.5).then_inc(consts, 1)
                nc.gpsimd.memset(half_power[:, XH:2 * XH], 0.5).then_inc(consts, 1)
                pool.wait_ge(pool_chain, 2)
                nc.gpsimd.affine_select(out=keep["identity"][:], in_=keep["identity"][:], compare_op=ALU.not_equal,
                                        fill=1.0, base=0, pattern=[[-1, P]], channel_multiplier=1).then_inc(consts, 1)
                nc.gpsimd.affine_select(out=tail_mask[:], in_=tail_mask[:], compare_op=ALU.is_gt, fill=NEG,
                                        base=P - DCA, pattern=[[0, 1]], channel_multiplier=-1).then_inc(consts, 1)
                pool.wait_ge(consts, 4)
                pool.wait_ge(var_ready, 1)
                nc.gpsimd.tensor_tensor(small[:, 8:12], small[:, 0:4], half_power[:, 0:4], ALU.pow).then_inc(rstd_ready, 1)
                for m in range(TM):
                    pool.wait_ge(var_ready, m + 2)
                    nc.gpsimd.tensor_tensor(small[:, 48:64], small[:, 32:48], half_power[:, 0:XH], ALU.pow).then_inc(rstd_ready, 1)
                pool.wait_ge(bound_var, 1)
                nc.gpsimd.tensor_tensor(small[:, 64:80], bound[:], half_power[:, XH:2 * XH], ALU.pow).then_inc(bound_ready, 1)

            @block.scalar
            def _(act):
                act.dma_start(bq_row[:], broadcast_rows(io["bq"], P)).then_inc(in_w, 16)
                act.dma_start(qn_w[:], broadcast_rows(io["qn_w"], P)).then_inc(in_w, 16)
                act.dma_start(qn_b[:], broadcast_rows(io["qn_b"], P)).then_inc(in_w, 16)
                for j in range(2):
                    act.dma_start(kn_col[j * XD:(j + 1) * XD, :], io["kn_w"].rearrange("(d o) -> d o", o=1)).then_inc(in_w, 16)
                act.dma_start(bk_raw[:], io["bk"]).then_inc(in_w, 16)
                act.dma_start(keep["bias_v"][:, 0:PAIRS], io["bv"]).then_inc(in_w, 16)
                for k in range(DK):
                    act.wait_ge(in_wq[k % 2], 16 * (k // 2 + 1))
                    nc.scalar.activation(wq_hi[:, k, :], wq_raw[:, k % 2, :], ACT.Copy).then_inc(wq_hi_ready, 1)
                    if k >= 4:
                        x_hi(act, k - 4)
                for k in range(4, DK):
                    x_hi(act, k)
                for p in range(PAIRS):
                    act.wait_ge(qt_banked, p + 1)
                    nc.scalar.activation(keep["q_t"][:, p, :], bank[p % 2][:], ACT.Copy).then_inc(qt_copied, 1)
                    if p == 0:
                        act.wait_ge(in_w, 7 * 16)
                        act.wait_ge(a_chain, 1)
                    if p >= 2:
                        act.wait_ge(q_lo_ready, p - 1)
                        act.wait_ge(sq_ready, p - 1)
                    nc.scalar.activation(qk[:, p % 2, :], bank[p % 2][:], ACT.Copy, scale=small[:, 80:81]).then_inc(qk_ready, 1)
                    act.wait_ge(qk_ready, p + 1)
                    if p >= 2:
                        act.wait_ge(q_stored[p % 2], 32 * (p // 2))
                        act.wait_ge(norm_banked, 2 * (p - 1))
                    nc.scalar.activation(q_hi[:, p % 2, :], qk[:, p % 2, :], ACT.Copy).then_inc(q_hi_ready, 1)
                    nc.scalar.activation(square[:, (p % 2) * TOK:(p % 2 + 1) * TOK], qk[:, p % 2, :], ACT.Square).then_inc(sq_ready, 1)

            @block.vector
            def _(dve):
                links = [0]

                def link(ins):
                    links[0] += 1
                    ins.then_inc(v_chain, 1)
                    dve.wait_ge(v_chain, links[0])

                link(nc.vector.memset(head_mean[:], 0.0))
                link(nc.vector.memset(head_ones[:], 0.0))
                for j in range(2):
                    rows = slice(j * XD, (j + 1) * XD)
                    link(nc.vector.memset(head_mean[rows, rows], 1.0 / XD))
                    link(nc.vector.memset(head_ones[rows, j, :], 1.0))
                dve.sem_inc(consts, 1)
                for m in range(TM):
                    if m == 0:
                        dve.wait_ge(in_x, 16 * TM)
                    for s in range(2):
                        link(nc.vector.bn_stats(stats[:, m, s, :], x_sb[:, m, s * 512:(s + 1) * 512]))
                    link(nc.vector.bn_aggr(means[:, m, :], stats[:, m, :, :]))
                nc.vector.tensor_scalar(small[:, 0:4], means[:, :, 1], 1e-5, None, ALU.add).then_inc(var_ready, 1)
                dve.wait_ge(rstd_ready, 1)
                for m in range(TM):
                    nc.vector.tensor_scalar(xn[:, m, :], x_sb[:, m, :], means[:, m, 0:1], small[:, 8 + m:9 + m],
                                            ALU.subtract, ALU.mult).then_inc(xn_ready, 1)
                dve.wait_ge(in_w, 7 * 16)
                nc.vector.tensor_scalar(small[:, 80:81], kn_col[:], XSCALE, None, ALU.mult).then_inc(a_chain, 1)
                for k in range(DK):
                    dve.wait_ge(wq_hi_ready, k + 1)
                    nc.vector.tensor_tensor(wq_lo[:, k, :], wq_raw[:, k % 2, :], wq_hi[:, k, :].bitcast(F32),
                                            ALU.subtract).then_inc(wq_lo_ready, 1)
                    if k >= 4:
                        x_lo(dve, k - 4)
                for k in range(4, DK):
                    x_lo(dve, k)
                for m in range(TM):
                    for h in range(2):
                        n = 2 * m + h
                        dve.wait_ge(q_banked, n + 1)
                        nc.vector.tensor_tensor(q[:, m, h * 512:(h + 1) * 512], bank[4 + n % 4][:],
                                                bq_row[:, h * 512:(h + 1) * 512], ALU.add).then_inc(q_taken, 1)
                    dve.wait_ge(q_taken, 2 * m + 2)
                    heads = q[:, m, :].rearrange("p (h d) -> p h d", h=XH)
                    sq3 = square[:, :].rearrange("p (h d) -> p h d", h=XH)
                    per_head = lambda a: small[:, a:a + XH].rearrange("p (h o) -> p h o", o=1).broadcast_to([P, XH, XD])
                    per_dim = lambda v: v[:, :].rearrange("p (o d) -> p o d", o=1).broadcast_to([P, XH, XD])
                    link(nc.vector.tensor_reduce(small[:, 16:32], heads, AX.X, ALU.add))
                    link(nc.vector.tensor_scalar(small[:, 16:32], small[:, 16:32], 1.0 / XD, None, ALU.mult))
                    link(nc.vector.tensor_tensor(heads, heads, per_head(16), ALU.subtract))
                    link(nc.vector.tensor_tensor(sq3, heads, heads, ALU.mult))
                    link(nc.vector.tensor_reduce(small[:, 32:48], sq3, AX.X, ALU.add))
                    link(nc.vector.tensor_scalar(small[:, 32:48], small[:, 32:48], 1.0 / XD, 1e-6, ALU.mult, ALU.add))
                    dve.sem_inc(var_ready, 1)
                    dve.wait_ge(rstd_ready, m + 2)
                    link(nc.vector.tensor_tensor(heads, heads, per_head(48), ALU.mult))
                    link(nc.vector.tensor_tensor(heads, heads, per_dim(qn_w), ALU.mult))
                    nc.vector.tensor_tensor(heads, heads, per_dim(qn_b), ALU.add).then_inc(q_ready, 1)
                dve.wait_ge(bmean_banked, 1)
                link(nc.vector.tensor_tensor(keep["bias_k"][:, 0:PAIRS], bank[2][:, 0:PAIRS], bk_raw[:], ALU.subtract))
                link(nc.vector.tensor_scalar(keep["bias_k"][:, 0:PAIRS], keep["bias_k"][:, 0:PAIRS], -1.0, None, ALU.mult))
                link(nc.vector.tensor_copy(keep["bias_k"][:, PAIRS:PAIRS + 1], keep["bias_k"][:, 0:1]))
                link(nc.vector.tensor_copy(keep["bias_v"][:, PAIRS:PAIRS + 1], keep["bias_v"][:, 0:1]))
                for p in range(PAIRS):
                    dve.wait_ge(q_hi_ready, p + 1)
                    if p >= 2:
                        dve.wait_ge(q_stored[p % 2], 32 * (p // 2))
                    nc.vector.tensor_tensor(q_lo[:, p % 2, :], qk[:, p % 2, :], q_hi[:, p % 2, :].bitcast(F32),
                                            ALU.subtract).then_inc(q_lo_ready, 1)
                    for j in range(2):
                        dve.wait_ge(norm_banked, 2 * p + j + 1)
                        nc.vector.tensor_reduce(bound[:, 2 * p + j:2 * p + j + 1], bank[4 + j][:], AX.X, ALU.max).then_inc(norm_taken, 1)
                dve.wait_ge(norm_taken, XH)
                dve.sem_inc(bound_var, 1)
                dve.wait_ge(bound_ready, 1)
                link(nc.vector.tensor_scalar(small[:, 96:112], small[:, 64:80], -float(XD) ** 0.5, RANGE, ALU.mult, ALU.add))
                guard = keep["guard"]
                link(nc.vector.memset(guard[:], 0.0))
                link(nc.vector.tensor_scalar(guard[:, 0:XH, 0], small[:, 96:112], 0.0, None, ALU.min))
                link(nc.vector.tensor_scalar(guard[:, :, 1], guard[:, :, 0], tail_mask[:, 0:1], None, ALU.add))

            @block.tensor
            def _(pe):
                pe.wait_ge(consts, 5)
                pe.wait_ge(xn_ready, TM)
                for k in range(DK):
                    if k >= 4:
                        pe.wait_ge(xt_lo_ready, k - 3)
                    for m in range(TM):
                        last = nc.tensor.transpose(bank[k % 4][:, m * P:(m + 1) * P], xn[:, m, k * P:(k + 1) * P], keep["identity"][:])
                    last.then_inc(xt_banked, 1)
                pe.wait_ge(in_w, 7 * 16)
                pe.wait_ge(xt_lo_ready, DK)
                nc.tensor.matmul(bank[2][:, 0:PAIRS], head_mean[:], bk_raw[:], start=True, stop=True).then_inc(bmean_banked, 1)
                pe.wait_ge(wq_lo_ready, DK)
                for m in range(TM):
                    for h in range(2):
                        n = 2 * m + h
                        if n >= 4:
                            pe.wait_ge(q_taken, n - 3)
                        for k in range(DK):
                            for a, (xs, ws) in enumerate([(xt_hi, wq_hi), (xt_hi, wq_lo), (xt_lo, wq_hi)]):
                                last = nc.tensor.matmul(bank[4 + n % 4][:], xs[:, k, m * P:(m + 1) * P], ws[:, k, h * 512:(h + 1) * 512],
                                                        start=(k == 0 and a == 0), stop=(k == DK - 1 and a == 2))
                        last.then_inc(q_banked, 1)
                pe.wait_ge(q_ready, TM)

                def norms(p):
                    pe.wait_ge(sq_ready, p + 1)
                    for j in range(2):
                        if p >= 1:
                            pe.wait_ge(norm_taken, 2 * (p - 1) + j + 1)
                        nc.tensor.matmul(bank[4 + j][:], head_ones[:, j, :], square[:, (p % 2) * TOK:(p % 2 + 1) * TOK],
                                         start=True, stop=True).then_inc(norm_banked, 1)

                for p in range(PAIRS):
                    if p >= 2:
                        pe.wait_ge(qk_ready, p - 1)
                    for m in range(TM):
                        last = nc.tensor.transpose(bank[p % 2][:, m * P:(m + 1) * P], q[:, m, p * P:(p + 1) * P], keep["identity"][:])
                    last.then_inc(qt_banked, 1)
                    if p >= 1:
                        norms(p - 1)
                norms(PAIRS - 1)


GROUPS = 2
GH = XH // GROUPS


def second_attention(nc, io, keep):
    with ExitStack() as ctx:
        def sb(name, shape, dt=F32):
            return ctx.enter_context(nc.sbuf_tensor("d_" + name, shape, dt))

        def sem(name):
            return nc.alloc_semaphore("d_" + name)

        rows_t = sb("rows_t", [P, CK, DCA])
        w = sb("w", [P, CK, 2 * D])
        bias = sb("bias", [DCA, 2 * D])
        norm_w = sb("norm_w", [DCA, XD])
        norm_b = sb("norm_b", [DCA, XD])
        kv = sb("kv", [DCA, 2 * D])
        sq = sb("sq", [DCA, D])
        stat = sb("stat", [DCA, 4, XH])
        power = sb("power", [DCA, XH])
        spread = sb("spread", [DCA, P])
        own_head = sb("own_head", [P, GH, XD])
        k_blocks = sb("k_blocks", [P, PAIRS, 2 * DCA])
        e = sb("e", [P, TM, XH, DCA])
        top = sb("top", [P, TM, XH])
        total = sb("total", [P, TM, XH])
        e_t = sb("e_t", [P, GROUPS, TOK])
        dca_t = sb("dca_out", [P, PAIRS, TOK])
        v_blocks = sb("v_blocks", [P, GROUPS, GH * XD])
        bank = [ctx.enter_context(nc.psum_tensor(f"d_bank{i}", [P, 512], F32)) for i in range(8)]

        in_all, consts, power_ready, pool_chain, v_chain = sem("in_all"), sem("consts"), sem("power_ready"), sem("pool_chain"), sem("v_chain")
        kv_banked, var_ready, rstd_ready, kv_ready = sem("kv_banked"), sem("var_ready"), sem("rstd_ready"), sem("kv_ready")
        k_turned, k_placed, scored, shifted, e_ready, e_norm, e_turned, e_placed = (sem(n) for n in (
            "k_turned", "k_placed", "scored", "shifted", "e_ready", "e_norm", "e_turned", "e_placed"))
        v_spread, v_placed, summed, out_ready, stored = sem("v_spread"), sem("v_placed"), sem("summed"), sem("out_ready"), sem("stored")
        identity = keep["identity"]

        with nc.Block() as block:
            @block.sync
            def _(sp):
                sp.dma_start(rows_t[:], io["dca_t"]).then_inc(in_all, 16)
                for k in range(CK):
                    sp.dma_start(w[:, k, :], io["wkv_dca"][k * P:(k + 1) * P, :]).then_inc(in_all, 16)
                sp.dma_start(bias[:], broadcast_rows(io["bkv_dca"], DCA)).then_inc(in_all, 16)
                sp.dma_start(norm_w[:], broadcast_rows(io["kn_dca_w"], DCA)).then_inc(in_all, 16)
                sp.dma_start(norm_b[:], broadcast_rows(io["kn_dca_b"], DCA)).then_inc(in_all, 16)
                sp.wait_ge(out_ready, PAIRS)
                sp.dma_start(keep["dca_dram"], dca_t[:]).then_inc(stored, 16)
                sp.wait_ge(stored, 16)

            @block.gpsimd
            def _(pool):
                nc.gpsimd.memset(power[:], -0.5).then_inc(power_ready, 1)
                nc.gpsimd.memset(spread[:], 0.0).then_inc(pool_chain, 1)
                nc.gpsimd.memset(own_head[:], 1.0).then_inc(pool_chain, 1)
                pool.wait_ge(pool_chain, 2)
                nc.gpsimd.affine_select(out=spread[:, :].rearrange("k (h r) -> k h r", r=DCA), in_=spread[:, :].rearrange("k (h r) -> k h r", r=DCA),
                                        compare_op=ALU.not_equal, fill=1.0, base=0, pattern=[[0, GH], [-1, DCA]], channel_multiplier=1).then_inc(consts, 1)
                nc.gpsimd.affine_select(out=own_head[:], in_=own_head[:], compare_op=ALU.is_ge, fill=0.0, base=0,
                                        pattern=[[-DCA, GH], [0, XD]], channel_multiplier=1).then_inc(pool_chain, 1)
                pool.wait_ge(pool_chain, 3)
                nc.gpsimd.affine_select(out=own_head[:], in_=own_head[:], compare_op=ALU.is_ge, fill=0.0, base=DCA - 1,
                                        pattern=[[DCA, GH], [0, XD]], channel_multiplier=-1).then_inc(consts, 1)
                pool.wait_ge(power_ready, 1)
                pool.wait_ge(var_ready, 1)
                nc.gpsimd.tensor_tensor(stat[:, 2, :], stat[:, 1, :], power[:], ALU.pow).then_inc(rstd_ready, 1)

            @block.scalar
            def _(act):
                for m in range(TM):
                    act.wait_ge(shifted, m + 1)
                    nc.scalar.activation(e[:, m, :, :], e[:, m, :, :], ACT.Exp, scale=XSCALE).then_inc(e_ready, 1)
                for p in range(PAIRS):
                    act.wait_ge(summed, p + 1)
                    nc.scalar.activation(dca_t[:, p, :], bank[p][:], ACT.Copy).then_inc(out_ready, 1)

            @block.vector
            def _(dve):
                links = [0]

                def link(ins):
                    links[0] += 1
                    ins.then_inc(v_chain, 1)
                    dve.wait_ge(v_chain, links[0])

                link(nc.vector.memset(k_blocks[:], 0.0))
                dve.wait_ge(in_all, 16 * (CK + 4))
                for c in range(4):
                    dve.wait_ge(kv_banked, c + 1)
                    link(nc.vector.tensor_tensor(kv[:, c * 512:(c + 1) * 512], bank[c][0:DCA, :], bias[:, c * 512:(c + 1) * 512], ALU.add))
                heads = kv[:, 0:D].rearrange("p (h d) -> p h d", h=XH)
                sq3 = sq[:, :].rearrange("p (h d) -> p h d", h=XH)
                per_head = lambda a: stat[:, a, :].rearrange("p (h o) -> p h o", o=1).broadcast_to([DCA, XH, XD])
                per_dim = lambda v: v[:, :].rearrange("p (o d) -> p o d", o=1).broadcast_to([DCA, XH, XD])
                link(nc.vector.tensor_reduce(stat[:, 0, :], heads, AX.X, ALU.add))
                link(nc.vector.tensor_scalar(stat[:, 0, :], stat[:, 0, :], 1.0 / XD, None, ALU.mult))
                link(nc.vector.tensor_tensor(heads, heads, per_head(0), ALU.subtract))
                link(nc.vector.tensor_tensor(sq3, heads, heads, ALU.mult))
                link(nc.vector.tensor_reduce(stat[:, 1, :], sq3, AX.X, ALU.add))
                nc.vector.tensor_scalar(stat[:, 1, :], stat[:, 1, :], 1.0 / XD, 1e-6, ALU.mult, ALU.add).then_inc(var_ready, 1)
                dve.wait_ge(rstd_ready, 1)
                link(nc.vector.tensor_tensor(heads, heads, per_head(2), ALU.mult))
                link(nc.vector.tensor_tensor(heads, heads, per_dim(norm_w), ALU.mult))
                nc.vector.tensor_tensor(heads, heads, per_dim(norm_b), ALU.add).then_inc(kv_ready, 1)
                dve.wait_ge(k_turned, 1)
                turned = bank[4][:, 0:PAIRS * DCA].rearrange("p (c r) -> p c r", r=DCA)
                for j in range(2):
                    rows = slice(j * XD, (j + 1) * XD)
                    nc.vector.tensor_copy(k_blocks[rows, :, j * DCA:(j + 1) * DCA], turned[rows, :, :]).then_inc(k_placed, 1)
                dve.wait_ge(consts, 2)
                for g in range(GROUPS):
                    dve.wait_ge(v_spread, g + 1)
                    nc.vector.tensor_tensor(v_blocks[:, g, :], bank[5 + g][:], own_head[:, :, :].rearrange("p h d -> p (h d)"), ALU.mult).then_inc(v_placed, 1)
                for m in range(TM):
                    dve.wait_ge(scored, m + 1)
                    s = bank[m][:, 0:XH * DCA].rearrange("p (h r) -> p h r", r=DCA)
                    per = lambda t: t[:, m, :].rearrange("p (h o) -> p h o", o=1).broadcast_to([P, XH, DCA])
                    link(nc.vector.tensor_reduce(top[:, m, :], s, AX.X, ALU.max))
                    nc.vector.tensor_tensor(e[:, m, :, :], s, per(top), ALU.subtract).then_inc(shifted, 1)
                for m in range(TM):
                    per = lambda t: t[:, m, :].rearrange("p (h o) -> p h o", o=1).broadcast_to([P, XH, DCA])
                    dve.wait_ge(e_ready, m + 1)
                    link(nc.vector.tensor_reduce(total[:, m, :], e[:, m, :, :], AX.X, ALU.add))
                    link(nc.vector.reciprocal(total[:, m, :], total[:, m, :]))
                    nc.vector.tensor_tensor(e[:, m, :, :], e[:, m, :, :], per(total), ALU.mult).then_inc(e_norm, 1)
                for g in range(GROUPS):
                    dve.wait_ge(e_turned, g + 1)
                    nc.vector.tensor_copy(e_t[:, g, :], bank[4 + g][:]).then_inc(e_placed, 1)

            @block.tensor
            def _(pe):
                pe.wait_ge(in_all, 16 * (CK + 4))
                for c in range(4):
                    for k in range(CK):
                        last = nc.tensor.matmul(bank[c][0:DCA, :], rows_t[:, k, :], w[:, k, c * 512:(c + 1) * 512], start=(k == 0), stop=(k == CK - 1))
                    last.then_inc(kv_banked, 1)
                pe.wait_ge(kv_ready, 1)
                for p in range(PAIRS):
                    last = nc.tensor.transpose(bank[4][:, p * DCA:(p + 1) * DCA], kv[:, p * P:(p + 1) * P], identity[0:DCA, 0:DCA])
                last.then_inc(k_turned, 1)
                pe.wait_ge(consts, 2)
                for g in range(GROUPS):
                    nc.tensor.matmul(bank[5 + g][:], spread[:], kv[:, D + g * 512:D + (g + 1) * 512], start=True, stop=True).then_inc(v_spread, 1)
                pe.wait_ge(k_placed, 2)
                for m in range(TM):
                    for p in range(PAIRS):
                        last = nc.tensor.matmul(bank[m][:, p * 2 * DCA:(p + 1) * 2 * DCA], keep["q_t"][:, p, m * P:(m + 1) * P], k_blocks[:, p, :], start=True, stop=True)
                    last.then_inc(scored, 1)
                pe.wait_ge(v_placed, GROUPS)
                pe.wait_ge(e_norm, TM)
                for g in range(GROUPS):
                    for m in range(TM):
                        last = nc.tensor.transpose(bank[4 + g][:, m * P:(m + 1) * P], e[:, m, g * GH:(g + 1) * GH, :].rearrange("p h r -> p (h r)"), identity[:])
                    last.then_inc(e_turned, 1)
                pe.wait_ge(e_placed, GROUPS)
                for p in range(PAIRS):
                    g, c = divmod(p, GH // 2)
                    nc.tensor.matmul(bank[p][:], v_blocks[:, g, c * P:(c + 1) * P], e_t[:, g, :], start=True, stop=True).then_inc(summed, 1)


PRING = 8
ERING = 4


def cross_attention(nc, io, keep):
    with ExitStack() as ctx:
        def sb(name, shape, dt=F32):
            return ctx.enter_context(nc.sbuf_tensor("a_" + name, shape, dt))

        def psum(name, shape, dt=F32):
            return ctx.enter_context(nc.psum_tensor("a_" + name, shape, dt))

        def sem(name):
            return nc.alloc_semaphore("a_" + name)

        raw = sb("raw", [P, 2, CK, CHUNK])
        c_hi = sb("c_hi", [P, 2, CK, CHUNK], F32R)
        c_lo = sb("c_lo", [P, 2, CK, CHUNK], F32R)
        w_raw = sb("w_raw", [P, 2, CK, P])
        wk_mid = sb("wk_mid", [P, CK, P])
        w_mean = sb("w_mean", [P, 2 * CK])
        w_hi = sb("w_hi", [P, 2, CK, P], F32R)
        w_lo = sb("w_lo", [P, 2, CK, P], F32R)
        bias_kp = sb("bias_kp", [P, 1])
        bias_vp = sb("bias_vp", [P, 1])
        guard_p = sb("guard_p", [P, 2, 2])
        q_hi = sb("q_hi", [P, 2, TOK], F32R)
        q_lo = sb("q_lo", [P, 2, TOK], F32R)
        k_f = sb("k_f", [P, CHUNK])
        v_f = sb("v_f", [P, CHUNK])
        k_split = sb("k_split", [P, 2, 2, CHUNK], F32R)
        k_sq = sb("k_sq", [P, CHUNK])
        var = sb("var", [P, 2 * KT])
        power = sb("power", [P, 2 * KT])
        rstd = sb("rstd", [P, 2, KT, 2])
        v_split = sb("v_split", [P, 2, KT, 2, 2 * XD + 1], F32R)
        ones_col = sb("ones_col", [P, XD + 1], F32R)
        e_f = sb("e_f", [P, ERING, TOK])
        e_hi = sb("e_hi", [P, PRING, TOK], F32R)
        e_lo = sb("e_lo", [P, PRING, TOK], F32R)
        o_pair = sb("o_pair", [P, TOK])
        sum_pair = sb("sum_pair", [P, 2, TOK])

        score = [psum(f"score{i}", [P, TOK]) for i in range(2)]
        proj = psum("proj", [P, CHUNK])
        turned = psum("turned", [P, CHUNK])
        acc = [psum(f"acc{i}", [P, TOK]) for i in range(2)]
        rest = [psum(f"rest{i}", [P, TOK]) for i in range(2)]

        in_raw = [sem(f"in_raw{i}") for i in range(2)]
        in_w = sem("in_w")
        in_q = [sem(f"in_q{i}") for i in range(2)]
        hi_done, lo_done = sem("hi_done"), sem("lo_done")
        wk_ready, wv_ready, w_chain, ones_ready = sem("wk_ready"), sem("wv_ready"), sem("w_chain"), sem("ones_ready")
        zeros_ready, power_ready = sem("zeros_ready"), sem("power_ready")
        k_proj, v_proj, kf_ready, vf_ready = sem("k_proj"), sem("v_proj"), sem("kf_ready"), sem("vf_ready")
        k_turned, v_turned = sem("k_turned"), sem("v_turned")
        k_hi_ready, k_lo_ready, sq_ready = sem("k_hi_ready"), sem("k_lo_ready"), sem("sq_ready")
        ssq_ready, var_ready, rstd_ready = sem("ssq_ready"), sem("var_ready"), sem("rstd_ready")
        v_hi_ready, v_lo_ready = sem("v_hi_ready"), sem("v_lo_ready")
        scored, e_ready, e_hi_ready, e_lo_ready, summed = sem("scored"), sem("e_ready"), sem("e_hi_ready"), sem("e_lo_ready"), sem("summed")
        bias_k_ready, bias_v_ready = sem("bias_k_ready"), sem("bias_v_ready")
        guard_ready = [sem(f"guard_ready{i}") for i in range(2)]
        o_part, o_ready = sem("o_part"), sem("o_ready")
        o_stored = [sem(f"o_stored{i}") for i in range(2)]

        identity = keep["identity"]
        LAST = PAIRS - 1


        def load_chunk(sp, t, c, b):
            sp.dma_start(raw[:, b, :, :], io["ctx_t"][bass.ds(c, 1), :, :, :].rearrange("o p k n -> p (o k) n")).then_inc(in_raw[b], 16)

        def load_q(sp, p, j):
            rows = keep["q_dram"][bass.ds(p, 1), j * XD:(j + 1) * XD, :, :].rearrange("o p s n -> (o p) s n").bitcast(F32)
            for half in range(2):
                for part, tile in enumerate((q_hi, q_lo)):
                    sp.dma_start(tile[half * XD:(half + 1) * XD, j, :].bitcast(F32), rows[:, part, :]).then_inc(in_q[j], 16)

        def load_w(sp, p):
            sp.dma_start(w_raw[:], io["wkv"][bass.ds(p, 1), :, :, :, :].rearrange("o p s k n -> p (o s) k n")).then_inc(in_w, 16)

        def split_w(dve, p, s):
            if s == 0:
                dve.wait_ge(in_w, 16 * (p + 1))
                heads = w_raw[:, 0, :, :].rearrange("p k (j d) -> p (k j) d", j=2)
                mid = wk_mid[:, :, :].rearrange("p k (j d) -> p (k j) d", j=2)
                mean = w_mean[:, :].rearrange("p (h o) -> p h o", o=1).broadcast_to([P, 2 * CK, XD])
                nc.vector.tensor_reduce(w_mean[:], heads, AX.X, ALU.add).then_inc(w_chain, 1)
                dve.wait_ge(w_chain, 4 * p + 1)
                nc.vector.tensor_scalar(w_mean[:], w_mean[:], 1.0 / XD, None, ALU.mult).then_inc(w_chain, 1)
                dve.wait_ge(w_chain, 4 * p + 2)
                nc.vector.tensor_tensor(mid, heads, mean, ALU.subtract).then_inc(w_chain, 1)
                dve.wait_ge(w_chain, 4 * p + 3)
                nc.vector.tensor_copy(w_hi[:, 0, :, :], wk_mid[:]).then_inc(w_chain, 1)
                dve.wait_ge(w_chain, 4 * p + 4)
                nc.vector.tensor_tensor(w_lo[:, 0, :, :], wk_mid[:], w_hi[:, 0, :, :].bitcast(F32), ALU.subtract).then_inc(wk_ready, 1)
            else:
                nc.vector.tensor_copy(w_hi[:, 1, :, :], w_raw[:, 1, :, :]).then_inc(wv_ready, 1)
                dve.wait_ge(wv_ready, 2 * p + 1)
                nc.vector.tensor_tensor(w_lo[:, 1, :, :], w_raw[:, 1, :, :], w_hi[:, 1, :, :].bitcast(F32), ALU.subtract).then_inc(wv_ready, 1)

        def chunk_hi(act, t, b, k):
            nc.scalar.activation(c_hi[:, b, k, :], raw[:, b, k, :], ACT.Copy).then_inc(hi_done, 1)

        def chunk_hi_waits(act, t, b, first):
            act.wait_ge(in_raw[b], 16 * (t // 2 + 1) if isinstance(t, int) else 8 * (t - b) + 16)
            if not first:
                act.wait_ge(v_proj, t - 1)

        def chunk_lo(pool, t, b):
            for k in range(CK):
                pool.wait_ge(hi_done, 4 * t + k + 1)
                nc.gpsimd.tensor_tensor(c_lo[:, b, k, :], raw[:, b, k, :], c_hi[:, b, k, :].bitcast(F32), ALU.subtract).then_inc(lo_done, 1)

        def pe_proj(pe, s, b, part):
            todo = [(k, a) for k in range(CK) for a in range(3)][4 * part:4 * part + 4]
            for k, a in todo:
                w, c = [(w_hi, c_hi), (w_lo, c_hi), (w_hi, c_lo)][a]
                last = nc.tensor.matmul(proj[:], w[:, s, k, :], c[:, b, k, :], start=(k == 0 and a == 0), stop=(k == CK - 1 and a == 2))
            if part == 2:
                last.then_inc(v_proj if s else k_proj, 1)

        def pe_turn(pe, s):
            for i in range(KT):
                last = nc.tensor.transpose(turned[:, i * P:(i + 1) * P], (v_f if s else k_f)[:, i * P:(i + 1) * P], identity[:])
            last.then_inc(v_turned if s else k_turned, 1)

        def pe_score(pe, g, b, j, i, waits=True):
            if waits:
                pe.wait_ge(e_ready, g - 1)
            for a, q in enumerate((q_hi, q_lo)):
                last = nc.tensor.matmul(score[i % 2][:], k_split[:, b, j, i * P:(i + 1) * P], q[:, j, :], start=(a == 0), stop=(a == 1))
            last.then_inc(scored, 1)

        def pe_sum(pe, g, b, j, i, start, stop):
            slot = 4 * j + i
            pe.wait_ge(e_lo_ready, g + 1)
            nc.tensor.matmul(acc[j][:], v_split[:, b, i, j, 0:2 * XD], e_hi[:, slot, :], start=start, stop=stop)
            nc.tensor.matmul(rest[j][0:XD + 1, :], v_split[:, b, i, j, XD:2 * XD + 1], e_lo[:, slot, :], start=start, stop=False)
            nc.tensor.matmul(rest[j][0:XD + 1, :], ones_col[:], e_hi[:, slot, :], start=False, stop=stop).then_inc(summed, 1)

        def act_kf(act, t, first):
            act.wait_ge(k_proj, t + 1)
            if not first:
                act.wait_ge(k_turned, t)
                act.wait_ge(k_hi_ready, 2 * t)
                act.wait_ge(k_lo_ready, 2 * t)
            nc.scalar.activation(k_f[:], proj[:], ACT.Identity, bias=bias_kp[:]).then_inc(kf_ready, 1)

        def act_vf(act, t, first):
            act.wait_ge(v_proj, t + 1)
            if not first:
                act.wait_ge(v_turned, t)
            nc.scalar.activation(v_f[:], proj[:], ACT.Identity, bias=bias_vp[:]).then_inc(vf_ready, 1)

        def act_k_hi(act, t, b):
            act.wait_ge(kf_ready, t + 1)
            for j in range(2):
                rows = slice(j * XD, (j + 1) * XD)
                nc.scalar.activation(k_split[rows, b, j, :], k_f[rows, :], ACT.Copy).then_inc(k_hi_ready, 1)

        def act_k_sq(act, t, first):
            act.wait_ge(k_turned, t + 1)
            if not first:
                act.wait_ge(ssq_ready, t)
            nc.scalar.activation(k_sq[:], turned[:], ACT.Square).then_inc(sq_ready, 1)

        def act_exp(act, g, b, j, i, tail, waits=True):
            act.wait_ge(scored, g + 1)
            if waits:
                act.wait_ge(e_lo_ready, g - ERING + 1)
            mask = 1 if tail and i == KT - 1 else 0
            nc.scalar.activation(e_f[:, i, :], score[i % 2][:], ACT.Exp, bias=guard_p[:, j, mask:mask + 1],
                                 scale=rstd[:, b, i, j:j + 1]).then_inc(e_ready, 1)

        def dve_e_hi(dve, g, j, i, waits=True):
            slot = 4 * j + i
            dve.wait_ge(e_ready, g + 1)
            if waits:
                dve.wait_ge(summed, g + 1)
            nc.vector.tensor_copy(e_hi[:, slot, :], e_f[:, i, :]).then_inc(e_hi_ready, 1)

        def dve_e_lo(dve, g, j, i):
            slot = 4 * j + i
            dve.wait_ge(e_hi_ready, g + 1)
            nc.vector.tensor_tensor(e_lo[:, slot, :], e_f[:, i, :], e_hi[:, slot, :].bitcast(F32), ALU.subtract).then_inc(e_lo_ready, 1)

        def dve_k_lo(dve, t, b):
            dve.wait_ge(k_hi_ready, 2 * t + 2)
            for j in range(2):
                rows, other = slice(j * XD, (j + 1) * XD), slice((1 - j) * XD, (2 - j) * XD)
                nc.vector.tensor_tensor(k_split[other, b, j, :], k_f[rows, :], k_split[rows, b, j, :].bitcast(F32), ALU.subtract).then_inc(k_lo_ready, 1)

        def dve_var(dve, t, first):
            dve.wait_ge(sq_ready, t + 1)
            if not first:
                dve.wait_ge(rstd_ready, t)
            nc.vector.tensor_reduce(var[:], k_sq[:, :].rearrange("p (h d) -> p h d", d=XD), AX.X, ALU.add).then_inc(ssq_ready, 1)
            dve.wait_ge(ssq_ready, t + 1)
            nc.vector.tensor_scalar(var[:], var[:], 1.0 / XD, 1e-6, ALU.mult, ALU.add).then_inc(var_ready, 1)

        def dve_v(dve, t, b, sums_before):
            dve.wait_ge(v_turned, t + 1)
            if sums_before is not None:
                dve.wait_ge(summed, PRING + sums_before)
            src = turned[:, :].rearrange("p (i j d) -> p (i j) d", j=2, d=XD)
            parts = v_split[:, b, :, :, :].rearrange("p i j c -> p (i j) c")
            nc.vector.tensor_copy(parts[:, :, XD:2 * XD], src).then_inc(v_hi_ready, 1)
            dve.wait_ge(v_hi_ready, t + 1)
            nc.vector.tensor_tensor(parts[:, :, 0:XD], src, parts[:, :, XD:2 * XD].bitcast(F32), ALU.subtract).then_inc(v_lo_ready, 1)

        def dve_finish(dve, p, j, n_next):
            rows, other = slice(j * XD, (j + 1) * XD), slice((1 - j) * XD, (2 - j) * XD)
            dve.wait_ge(summed, PRING + n_next)
            dve.wait_ge(o_stored[j], 32 * p + 32)
            nc.vector.tensor_copy(o_pair[rows, :], acc[j][rows, :]).then_inc(o_part, 1)
            nc.vector.tensor_copy(sum_pair[XD:XD + 1, j, :], rest[j][XD:XD + 1, :]).then_inc(o_part, 1)
            dve.wait_ge(o_part, 6 * p + 3 * j + 1)
            nc.vector.tensor_tensor(o_pair[rows, :], acc[j][other, :], o_pair[rows, :], ALU.add).then_inc(o_part, 1)
            dve.wait_ge(o_part, 6 * p + 3 * j + 3)
            nc.vector.tensor_tensor(o_pair[rows, :], rest[j][0:XD, :], o_pair[rows, :], ALU.add).then_inc(o_ready, 1)

        def store_o(sp, p, j):
            sp.wait_ge(o_ready, 2 * p + j + 3)
            sp.dma_start(keep["o_dram"][bass.ds(p, 1), j * XD:(j + 1) * XD, :].rearrange("o p n -> (o p) n"), o_pair[j * XD:(j + 1) * XD, :]).then_inc(o_stored[j], 16)
            sp.dma_start(keep["sum_dram"][bass.ds(2 * p + j, 1), :], sum_pair[XD:XD + 1, j, :]).then_inc(o_stored[j], 16)


        def pe_steps(pe, p, t, first, last):
            for u in range(2):
                for j in range(2):
                    n = 2 * t + 2 * u + j
                    for i in range(KT):
                        nb, nj = (u, 1) if j == 0 else (1 - u, 0)
                        if i == 0:
                            if j == 1:
                                pe.wait_ge(k_hi_ready, 2 * (t + u) + 4)
                                pe.wait_ge(k_lo_ready, 2 * (t + u) + 4)
                            if last and u == 1 and j == 1:
                                pe.wait_ge(in_q[0], 64 * p + 128)
                            if first and u == 0 and j == 0:
                                pe.wait_ge(in_q[1], 64 * p + 64)
                        pe_score(pe, 4 * n + 4 + i, nb, nj, i)
                        if i == 1 and j == 0:
                            pe.wait_ge(kf_ready, t + u + 2)
                            pe.wait_ge(v_lo_ready, t + u + 1)
                            pe_turn(pe, 0)
                            if last and u == 1:
                                pe.wait_ge(wv_ready, 2 * p + 4)
                        if i == 1 and j == 1:
                            pe.wait_ge(vf_ready, t + u + 2)
                            pe.wait_ge(sq_ready, t + u + 2)
                            pe_turn(pe, 1)
                            pe.wait_ge(lo_done, CK * (t + u + 3))
                            if last and u == 0:
                                pe.wait_ge(wk_ready, p + 2)
                        if i >= 1:
                            pe_proj(pe, 1 - j, (1 - u) if j == 0 else u, i - 1)
                        if i == 0 and j == 0:
                            pe.wait_ge(v_lo_ready, t + u + 1)
                        if first and u == 0 and i == 0:
                            finished_before(pe, p, j)
                        pe_sum(pe, 4 * n + i, u, j, i, start=(first and u == 0 and i == 0), stop=(last and u == 1 and i == KT - 1))

        def finished_before(pe, p, j):
            pe.wait_ge(o_ready, 2 * p + j + 1)

        def act_steps(act, p, t, first, last):
            for u in range(2):
                for j in range(2):
                    n = 2 * t + 2 * u + j
                    nb, nj = (u, 1) if j == 0 else (1 - u, 0)
                    tail = (last and u == 1 and j == 0) or (last and u == 0 and j == 1)
                    if j == 0:
                        act_kf_in_loop(act, p, t + u + 1, last and u == 1)
                    else:
                        act_vf_in_loop(act, p, t + u + 1, last and u == 1)
                    for i in range(KT):
                        if i == 0:
                            if j == 1:
                                act.wait_ge(rstd_ready, t + u + 2)
                            if last and u == 1 and j == 1:
                                act.wait_ge(guard_ready[0], p + 2)
                            if first and u == 0 and j == 0:
                                act.wait_ge(guard_ready[1], p + 1)
                        act_exp(act, 4 * n + 4 + i, nb, nj, i, tail)
                        if j == 0:
                            if i == 0:
                                act_k_hi(act, t + u + 1, 1 - u)
                            if i == 1:
                                act_k_sq(act, t + u + 1, False)
                        else:
                            if i == 0:
                                chunk_hi_waits(act, t + u + 3, 1 - u, False)
                            chunk_hi(act, t + u + 3, 1 - u, i)
                    if last:
                        if u == 0 and j == 1:
                            nc.scalar.activation(bias_kp[:], keep["bias_k"][:, bass.ds(p + 1, 1)], ACT.Copy).then_inc(bias_k_ready, 1)
                        if u == 1 and j == 0:
                            nc.scalar.activation(bias_vp[:], keep["bias_v"][:, bass.ds(p + 1, 1)], ACT.Copy).then_inc(bias_v_ready, 1)
                        if u == 1:
                            nc.scalar.activation(guard_p[:, j, :], keep["guard"][:, bass.ds(2 * p + 2 + j, 1), :].rearrange("p o s -> p (o s)"), ACT.Copy).then_inc(guard_ready[j], 1)

        def act_kf_in_loop(act, p, t, next_pair):
            if next_pair:
                act.wait_ge(bias_k_ready, p + 2)
            act_kf(act, t, False)

        def act_vf_in_loop(act, p, t, next_pair):
            if next_pair:
                act.wait_ge(bias_v_ready, p + 2)
            act_vf(act, t, False)

        def dve_steps(dve, p, t, last):
            for u in range(2):
                for j in range(2):
                    n = 2 * t + 2 * u + j
                    nj = 1 - j
                    for i in range(KT):
                        dve_e_hi(dve, 4 * n + 4 + i, nj, i)
                        if i == 1 and j == 0:
                            dve_k_lo(dve, t + u + 1, 1 - u)
                        dve_e_lo(dve, 4 * n + 4 + i, nj, i)
                        if i == 2 and j == 0:
                            dve_var(dve, t + u + 1, False)
                        if i == 2 and j == 1:
                            dve_v(dve, t + u + 1, 1 - u, 8 * (t + u))
                        if last and u == 0 and i == 2:
                            if j == 0:
                                dve.wait_ge(k_proj, t + 2)
                                split_w(dve, p + 1, 0)
                            else:
                                dve.wait_ge(v_proj, t + 2)
                                split_w(dve, p + 1, 1)
                        if last and u == 1 and j == 1 and i == 1:
                            dve_finish(dve, p, 0, 128 * p + 124)

        def pool_steps(pool, t):
            for u in range(2):
                pool.wait_ge(var_ready, t + u + 2)
                pool.wait_ge(e_ready, 8 * (t + u) + 4)
                nc.gpsimd.tensor_tensor(rstd[:, 1 - u, :, :].rearrange("p i j -> p (i j)"), var[:], power[:], ALU.pow).then_inc(rstd_ready, 1)
                chunk_lo(pool, t + u + 3, 1 - u)

        with nc.Block() as block:
            @block.sync
            def _(sp):
                load_w(sp, 0)
                load_chunk(sp, 0, 0, 0)
                load_chunk(sp, 1, 1, 1)
                load_q(sp, 0, 0)
                load_q(sp, 0, 1)
                sp.wait_ge(lo_done, CK)
                load_chunk(sp, 2, 2, 0)
                with sp.Fori(0, PAIRS) as p:
                    sp.wait_ge(wv_ready, 2 * p + 2)
                    load_w(sp, p + 1)
                    with sp.Fori(0, STEPS // 2 - 2) as k:
                        for u in range(2):
                            sp.wait_ge(lo_done, CK * (STEPS * p + 2 * k + u + 2))
                            load_chunk(sp, None, 2 * k + 3 + u, 1 - u)
                    for u, chunk in enumerate((STEPS - 1, 0, 1, 2)):
                        sp.wait_ge(lo_done, CK * (STEPS * p + STEPS - 4 + u + 2))
                        load_chunk(sp, None, chunk, 1 - u % 2)
                    for j in range(2):
                        sp.wait_ge(scored, 128 * p + 124 + 4 * j)
                        load_q(sp, p + 1, j)
                    store_o(sp, p, 0)
                    store_o(sp, p, 1)
                for j in range(2):
                    sp.wait_ge(o_stored[j], 32 * (PAIRS + 1))
                    sp.wait_ge(in_q[j], 64 * (PAIRS + 1))
                sp.wait_ge(in_w, 16 * (PAIRS + 1))
                for b in range(2):
                    sp.wait_ge(in_raw[b], 16 * (STEPS * PAIRS // 2 + 2 - b))

            @block.gpsimd
            def _(pool):
                nc.gpsimd.memset(power[:], -0.5).then_inc(power_ready, 1)
                pool.wait_ge(power_ready, 1)
                chunk_lo(pool, 0, 0)
                chunk_lo(pool, 1, 1)
                pool.wait_ge(var_ready, 1)
                nc.gpsimd.tensor_tensor(rstd[:, 0, :, :].rearrange("p i j -> p (i j)"), var[:], power[:], ALU.pow).then_inc(rstd_ready, 1)
                chunk_lo(pool, 2, 0)
                with pool.Fori(0, PAIRS * STEPS, 2) as t:
                    pool_steps(pool, t)

            @block.scalar
            def _(act):
                nc.scalar.activation(bias_kp[:], keep["bias_k"][:, 0:1], ACT.Copy).then_inc(bias_k_ready, 1)
                nc.scalar.activation(bias_vp[:], keep["bias_v"][:, 0:1], ACT.Copy).then_inc(bias_v_ready, 1)
                for j in range(2):
                    nc.scalar.activation(guard_p[:, j, :], keep["guard"][:, j, :], ACT.Copy).then_inc(guard_ready[j], 1)
                act.wait_ge(bias_k_ready, 1)
                act.wait_ge(bias_v_ready, 1)
                for t in range(2):
                    chunk_hi_waits(act, t, t, True)
                    for k in range(CK):
                        chunk_hi(act, t, t, k)
                    if t == 0:
                        act_kf(act, 0, True)
                        act_k_hi(act, 0, 0)
                        act_k_sq(act, 0, True)
                        act_vf(act, 0, True)
                chunk_hi_waits(act, 2, 0, False)
                for k in range(CK):
                    chunk_hi(act, 2, 0, k)
                act.wait_ge(rstd_ready, 1)
                act.wait_ge(guard_ready[0], 1)
                for i in range(KT):
                    act_exp(act, i, 0, 0, i, False, waits=False)
                with act.Fori(0, PAIRS) as p:
                    act_steps(act, p, STEPS * p, True, False)
                    with act.Fori(1, STEPS // 2 - 1) as k:
                        act_steps(act, p, STEPS * p + 2 * k, False, False)
                    act_steps(act, p, STEPS * p + STEPS - 2, False, True)

            @block.vector
            def _(dve):
                nc.vector.memset(ones_col[:].bitcast(F32), 0.0).then_inc(zeros_ready, 1)
                for b in range(2):
                    nc.vector.memset(v_split[:, b, :, :, 2 * XD:2 * XD + 1].rearrange("p i j o -> p (i j) o").bitcast(F32), 1.0).then_inc(ones_ready, 1)
                dve.wait_ge(zeros_ready, 1)
                nc.vector.memset(ones_col[:, XD:XD + 1].bitcast(F32), 1.0).then_inc(ones_ready, 1)
                dve.sem_inc(o_ready, 2)
                for j in range(2):
                    dve.sem_inc(o_stored[j], 32)
                split_w(dve, 0, 0)
                split_w(dve, 0, 1)
                dve_k_lo(dve, 0, 0)
                dve_var(dve, 0, True)
                dve_v(dve, 0, 0, None)
                for i in range(KT):
                    dve_e_hi(dve, i, 0, i, waits=False)
                    dve_e_lo(dve, i, 0, i)
                with dve.Fori(0, PAIRS) as p:
                    with dve.Fori(0, STEPS // 2 - 1) as k:
                        dve_steps(dve, p, STEPS * p + 2 * k, False)
                    dve_steps(dve, p, STEPS * p + STEPS - 2, True)
                    dve_finish(dve, p, 1, 128 * p + 128)

            @block.tensor
            def _(pe):
                pe.wait_ge(ones_ready, 3)
                pe.sem_inc(summed, PRING)
                pe.wait_ge(wk_ready, 1)
                pe.wait_ge(wv_ready, 2)
                pe.wait_ge(lo_done, CK)
                for part in range(3):
                    pe_proj(pe, 0, 0, part)
                pe.wait_ge(kf_ready, 1)
                pe_turn(pe, 0)
                for part in range(3):
                    pe_proj(pe, 1, 0, part)
                pe.wait_ge(vf_ready, 1)
                pe.wait_ge(sq_ready, 1)
                pe_turn(pe, 1)
                pe.wait_ge(lo_done, 2 * CK)
                for part in range(3):
                    pe_proj(pe, 0, 1, part)
                pe.wait_ge(k_hi_ready, 2)
                pe.wait_ge(k_lo_ready, 2)
                pe.wait_ge(in_q[0], 64)
                for i in range(KT):
                    pe_score(pe, i, 0, 0, i, waits=(i >= 2))
                with pe.Fori(0, PAIRS) as p:
                    pe_steps(pe, p, STEPS * p, True, False)
                    with pe.Fori(1, STEPS // 2 - 1) as k:
                        pe_steps(pe, p, STEPS * p + 2 * k, False, False)
                    pe_steps(pe, p, STEPS * p + STEPS - 2, False, True)


def combine_attentions(nc, io, keep):
    with ExitStack() as ctx:
        def sb(name, shape, dt=F32):
            return ctx.enter_context(nc.sbuf_tensor("c_" + name, shape, dt))

        def sem(name):
            return nc.alloc_semaphore("c_" + name)

        o = sb("o", [P, PAIRS, TOK])
        den = sb("den", [P, PAIRS, TOK])
        dca_t = sb("dca", [P, PAIRS, TOK])
        in_o, inverted, scaled, added, hi_ready, lo_ready = (sem(n) for n in ("in_o", "inverted", "scaled", "added", "hi_ready", "lo_ready"))

        with nc.Block() as block:
            def low(dve, p):
                dve.wait_ge(hi_ready, p + 1)
                nc.vector.tensor_tensor(keep["a_lo"][:, p, :], o[:, p, :], keep["a_hi"][:, p, :].bitcast(F32), ALU.subtract).then_inc(lo_ready, 1)

            @block.sync
            def _(sp):
                sums = keep["sum_dram"].rearrange("(p j) n -> j p n", j=2)
                for j in range(2):
                    sp.dma_start(den[j * XD:(j + 1) * XD, :, :], sums[j:j + 1, :, :].broadcast_to([XD, PAIRS, TOK])).then_inc(in_o, 16)
                sp.dma_start(dca_t[:], keep["dca_dram"]).then_inc(in_o, 16)
                sp.dma_start(o[:], keep["o_dram"].rearrange("p r n -> r p n")).then_inc(in_o, 16)

            @block.vector
            def _(dve):
                dve.wait_ge(in_o, 64)
                for p in range(PAIRS):
                    nc.vector.reciprocal(den[:, p, :], den[:, p, :]).then_inc(inverted, 1)
                    dve.wait_ge(inverted, p + 1)
                    nc.vector.tensor_tensor(o[:, p, :], o[:, p, :], den[:, p, :], ALU.mult).then_inc(scaled, 1)
                    dve.wait_ge(scaled, p + 1)
                    nc.vector.tensor_tensor(o[:, p, :], o[:, p, :], dca_t[:, p, :], ALU.add).then_inc(added, 1)
                    if p >= 1:
                        low(dve, p - 1)
                low(dve, PAIRS - 1)

            @block.scalar
            def _(act):
                for p in range(PAIRS):
                    act.wait_ge(added, p + 1)
                    nc.scalar.activation(keep["a_hi"][:, p, :], o[:, p, :], ACT.Copy).then_inc(hi_ready, 1)


def project_and_norm(nc, name, w_dram, bias, residual, keep):
    W = 4
    with ExitStack() as ctx:
        def sb(n, shape, dt=F32):
            return ctx.enter_context(nc.sbuf_tensor(f"{name}_{n}", shape, dt))

        def sem(n):
            return nc.alloc_semaphore(f"{name}_{n}")

        w_raw = sb("w_raw", [P, W, D])
        w_hi = sb("w_hi", [P, W, D], F32R)
        w_lo = sb("w_lo", [P, W, D], F32R)
        xn = sb("xn", [P, TM, D])
        stats = sb("stats", [P, TM, 2, 6])
        means = sb("means", [P, TM, 2])
        var = sb("var", [P, TM])
        power = sb("power", [P, TM])
        rstd = sb("rstd", [P, TM])
        bias_row = sb("bias_row", [P, D]) if bias is not None else None
        bank = [ctx.enter_context(nc.psum_tensor(f"{name}_bank{i}", [P, 512], F32)) for i in range(8)]

        in_w = [sem(f"in_w{i}") for i in range(W)]
        in_x, power_ready = sem("in_x"), sem("power_ready")
        hi_ready, lo_ready, multiplied = sem("hi_ready"), sem("lo_ready"), sem("multiplied")
        banked, biased, x_ready, stat_ready, mean_ready = sem("banked"), sem("biased"), sem("x_ready"), sem("stat_ready"), sem("mean_ready")
        var_ready, rstd_ready, xn_ready = sem("var_ready"), sem("rstd_ready"), sem("xn_ready")
        turned, t_hi_ready, t_lo_ready = sem("turned"), sem("t_hi_ready"), sem("t_lo_ready")
        x, xt_hi, xt_lo = keep["x"], keep["xt_hi"], keep["xt_lo"]
        n_in = (16 * TM if residual is not None else 0) + (16 if bias is not None else 0)

        with nc.Block() as block:
            @block.sync
            def _(sp):
                for k in range(DK):
                    if k >= W:
                        sp.wait_ge(hi_ready, k - W + 1)
                        sp.wait_ge(lo_ready, k - W + 1)
                    sp.dma_start(w_raw[:, k % W, :], w_dram[k * P:(k + 1) * P, :]).then_inc(in_w[k % W], 16)
                    if k == 1:
                        if residual is not None:
                            for m in range(TM):
                                sp.dma_start(x[:, m, :], residual[m * P:(m + 1) * P, :]).then_inc(in_x, 16)
                        if bias is not None:
                            sp.dma_start(bias_row[:], broadcast_rows(bias, P)).then_inc(in_x, 16)

            @block.gpsimd
            def _(pool):
                nc.gpsimd.memset(power[:], -0.5).then_inc(power_ready, 1)
                pool.wait_ge(power_ready, 1)
                for m in range(TM):
                    pool.wait_ge(var_ready, m + 1)
                    nc.gpsimd.tensor_tensor(rstd[:, m:m + 1], var[:, m:m + 1], power[:, 0:1], ALU.pow).then_inc(rstd_ready, 1)

            @block.scalar
            def _(act):
                for k in range(DK):
                    act.wait_ge(in_w[k % W], 16 * (k // W + 1))
                    if k >= W:
                        act.wait_ge(multiplied, k - W + 1)
                    nc.scalar.activation(w_hi[:, k % W, :], w_raw[:, k % W, :], ACT.Copy).then_inc(hi_ready, 1)
                for k in range(DK):
                    act.wait_ge(turned, k + 1)
                    nc.scalar.activation(xt_hi[:, k, :], bank[k][:], ACT.Copy).then_inc(t_hi_ready, 1)

            @block.vector
            def _(dve):
                for k in range(DK):
                    dve.wait_ge(hi_ready, k + 1)
                    nc.vector.tensor_tensor(w_lo[:, k % W, :], w_raw[:, k % W, :], w_hi[:, k % W, :].bitcast(F32), ALU.subtract).then_inc(lo_ready, 1)
                if n_in:
                    dve.wait_ge(in_x, n_in)
                if bias is not None:
                    for m in range(TM):
                        nc.vector.tensor_tensor(x[:, m, :], x[:, m, :], bias_row[:], ALU.add).then_inc(biased, 1)
                    dve.wait_ge(biased, TM)
                for m in range(TM):
                    for h in range(2):
                        n = 2 * m + h
                        cols = slice(h * 512, (h + 1) * 512)
                        dve.wait_ge(banked, n + 1)
                        nc.vector.tensor_tensor(x[:, m, cols], bank[n][:], x[:, m, cols], ALU.add).then_inc(x_ready, 1)
                        dve.wait_ge(x_ready, n + 1)
                        nc.vector.bn_stats(stats[:, m, h, :], x[:, m, cols]).then_inc(stat_ready, 1)
                    dve.wait_ge(stat_ready, 2 * m + 2)
                    nc.vector.bn_aggr(means[:, m, :], stats[:, m, :, :]).then_inc(mean_ready, 1)
                    dve.wait_ge(mean_ready, m + 1)
                    nc.vector.tensor_scalar(var[:, m:m + 1], means[:, m, 1:2], 1e-5, None, ALU.add).then_inc(var_ready, 1)
                for m in range(TM):
                    dve.wait_ge(rstd_ready, m + 1)
                    nc.vector.tensor_scalar(xn[:, m, :], x[:, m, :], means[:, m, 0:1], rstd[:, m:m + 1], ALU.subtract, ALU.mult).then_inc(xn_ready, 1)
                for k in range(DK):
                    dve.wait_ge(t_hi_ready, k + 1)
                    nc.vector.tensor_tensor(xt_lo[:, k, :], bank[k][:], xt_hi[:, k, :].bitcast(F32), ALU.subtract).then_inc(t_lo_ready, 1)

            @block.tensor
            def _(pe):
                for k in range(DK):
                    pe.wait_ge(lo_ready, k + 1)
                    for n in range(2 * TM):
                        m, h = divmod(n, 2)
                        for a, (s, w) in enumerate([("a_hi", w_hi), ("a_hi", w_lo), ("a_lo", w_hi)]):
                            last = nc.tensor.matmul(bank[n][:], keep[s][:, k, m * P:(m + 1) * P], w[:, k % W, h * 512:(h + 1) * 512],
                                                    start=(k == 0 and a == 0), stop=(k == DK - 1 and a == 2))
                        if k == DK - 1:
                            last.then_inc(banked, 1)
                    if k < DK - 1:
                        last.then_inc(multiplied, 1)
                pe.wait_ge(x_ready, 2 * TM)
                pe.wait_ge(xn_ready, TM)
                for k in range(DK):
                    for m in range(TM):
                        last = nc.tensor.transpose(bank[k][:, m * P:(m + 1) * P], xn[:, m, k * P:(k + 1) * P], keep["identity"][:])
                    last.then_inc(turned, 1)


SH, SKV = 32, 8
SD = D // SH
REP = SH // SKV
QB, KB = D // P, SKV * SD // P
SSCALE = 1.0 / float(SD) ** 0.5
MASKED = -10000000000.0 / SSCALE


def project_qkv(nc, io, keep):
    with ExitStack() as ctx:
        def sb(n, shape, dt=F32):
            return ctx.enter_context(nc.sbuf_tensor("j_" + n, shape, dt))

        def sem(n):
            return nc.alloc_semaphore("j_" + n)

        w_raw = sb("w_raw", [P, 2, DK, P])
        w_hi = sb("w_hi", [P, 2, DK, P], F32R)
        w_lo = sb("w_lo", [P, 2, DK, P], F32R)
        v_raw = sb("v_raw", [P, DK, SKV * SD])
        v_hi = sb("v_hi", [P, DK, SKV * SD], F32R)
        v_lo = sb("v_lo", [P, DK, SKV * SD], F32R)
        out_hi = sb("out_hi", [P, 2, TOK], F32R)
        out_lo = sb("out_lo", [P, 2, TOK], F32R)
        v_out = sb("v_out", [P, TM, SKV * SD])
        bank = [ctx.enter_context(nc.psum_tensor(f"j_bank{i}", [P, 512], F32)) for i in range(2)]
        v_bank = [ctx.enter_context(nc.psum_tensor(f"j_vbank{i}", [P, SKV * SD], F32)) for i in range(TM)]

        in_w = [sem(f"in_w{i}") for i in range(2)]
        in_v, vw_hi, vw_lo, v_banked, v_taken, v_stored = (sem(n) for n in ("in_v", "vw_hi", "vw_lo", "v_banked", "v_taken", "v_stored"))
        hi_ready, lo_ready, banked, out_hi_ready, out_lo_ready = (sem(n) for n in ("hi_ready", "lo_ready", "banked", "out_hi_ready", "out_lo_ready"))
        stored = [sem(f"stored{i}") for i in range(2)]
        xt_hi, xt_lo = keep["xt_hi"], keep["xt_lo"]
        BLOCKS = QB + KB

        def store(sp, b, i, count):
            sp.wait_ge(out_hi_ready, count)
            sp.wait_ge(out_lo_ready, count)
            dst = keep["qk_dram"][bass.ds(i, 1), :, :, :].rearrange("o p s n -> (o p) s n").bitcast(F32)
            sp.dma_start(dst[:, 0, :], out_hi[:, b, :].bitcast(F32)).then_inc(stored[b], 16)
            sp.dma_start(dst[:, 1, :], out_lo[:, b, :].bitcast(F32)).then_inc(stored[b], 16)

        with nc.Block() as block:
            @block.sync
            def _(sp):
                for b in range(2):
                    sp.dma_start(w_raw[:, b, :, :], io["wqk"][b, :, :, :]).then_inc(in_w[b], 16)
                sp.dma_start(v_raw[:], io["wv"].rearrange("(k p) n -> p k n", p=P)).then_inc(in_v, 16)
                for b in range(2):
                    sp.sem_inc(stored[b], 32)
                with sp.Fori(0, BLOCKS // 2 - 1) as i:
                    for b in range(2):
                        sp.wait_ge(hi_ready, 2 * i + b + 1)
                        sp.wait_ge(lo_ready, 2 * i + b + 1)
                        sp.dma_start(w_raw[:, b, :, :], io["wqk"][bass.ds(2 * i + b + 2, 1), :, :, :].rearrange("o p k n -> p (o k) n")).then_inc(in_w[b], 16)
                        store(sp, b, 2 * i + b, 2 * i + b + 1)
                for b in range(2):
                    store(sp, b, BLOCKS - 2 + b, BLOCKS - 1 + b)
                sp.wait_ge(v_taken, TM)
                sp.dma_start(keep["v_dram"].rearrange("m p n -> p m n"), v_out[:]).then_inc(v_stored, 16)
                for b in range(2):
                    sp.wait_ge(stored[b], 32 * (BLOCKS // 2 + 1))
                sp.wait_ge(v_stored, 16)

            @block.scalar
            def _(act):
                act.wait_ge(in_v, 16)
                nc.scalar.activation(v_hi[:], v_raw[:], ACT.Copy).then_inc(vw_hi, 1)

                def w_part(i, b):
                    act.wait_ge(in_w[b], 16 * i + 16)
                    nc.scalar.activation(w_hi[:, b, :, :], w_raw[:, b, :, :], ACT.Copy).then_inc(hi_ready, 1)

                def out_part(i, b):
                    act.wait_ge(banked, 2 * i + b + 1)
                    act.wait_ge(stored[b], 32 * i + 32)
                    nc.scalar.activation(out_hi[:, b, :], bank[b][:], ACT.Copy).then_inc(out_hi_ready, 1)

                for b in range(2):
                    w_part(0, b)
                with act.Fori(0, BLOCKS // 2 - 1) as i:
                    for b in range(2):
                        out_part(i, b)
                        w_part(i + 1, b)
                for b in range(2):
                    out_part(BLOCKS // 2 - 1, b)

            @block.vector
            def _(dve):
                dve.wait_ge(vw_hi, 1)
                nc.vector.tensor_tensor(v_lo[:], v_raw[:], v_hi[:].bitcast(F32), ALU.subtract).then_inc(vw_lo, 1)

                def w_part(i, b):
                    dve.wait_ge(hi_ready, 2 * i + b + 1)
                    nc.vector.tensor_tensor(w_lo[:, b, :, :], w_raw[:, b, :, :], w_hi[:, b, :, :].bitcast(F32), ALU.subtract).then_inc(lo_ready, 1)

                def out_part(i, b):
                    dve.wait_ge(out_hi_ready, 2 * i + b + 1)
                    nc.vector.tensor_tensor(out_lo[:, b, :], bank[b][:], out_hi[:, b, :].bitcast(F32), ALU.subtract).then_inc(out_lo_ready, 1)

                for b in range(2):
                    w_part(0, b)
                with dve.Fori(0, BLOCKS // 2 - 1) as i:
                    for b in range(2):
                        out_part(i, b)
                        w_part(i + 1, b)
                for b in range(2):
                    out_part(BLOCKS // 2 - 1, b)
                for m in range(TM):
                    dve.wait_ge(v_banked, m + 1)
                    nc.vector.tensor_copy(v_out[:, m, :], v_bank[m][:]).then_inc(v_taken, 1)

            @block.tensor
            def _(pe):
                def products(i, b, first):
                    pe.wait_ge(lo_ready, 2 * i + b + 1)
                    if not first:
                        pe.wait_ge(out_lo_ready, 2 * i + b - 1)
                    for k in range(DK):
                        for a, (w, x) in enumerate([(w_hi, xt_hi), (w_lo, xt_hi), (w_hi, xt_lo)]):
                            last = nc.tensor.matmul(bank[b][:], w[:, b, k, :], x[:, k, :], start=(k == 0 and a == 0), stop=(k == DK - 1 and a == 2))
                    last.then_inc(banked, 1)

                for b in range(2):
                    products(0, b, True)
                with pe.Fori(1, BLOCKS // 2) as i:
                    for b in range(2):
                        products(i, b, False)
                pe.wait_ge(vw_lo, 1)
                for m in range(TM):
                    for k in range(DK):
                        for a, (x, w) in enumerate([(xt_hi, v_hi), (xt_hi, v_lo), (xt_lo, v_hi)]):
                            last = nc.tensor.matmul(v_bank[m][:], x[:, k, m * P:(m + 1) * P], w[:, k, :], start=(k == 0 and a == 0), stop=(k == DK - 1 and a == 2))
                    last.then_inc(v_banked, 1)


def self_attention(nc, io, keep):
    with ExitStack() as ctx:
        def sb(n, shape, dt=F32):
            return ctx.enter_context(nc.sbuf_tensor("s_" + n, shape, dt))

        def sem(n):
            return nc.alloc_semaphore("s_" + n)

        q_st = sb("q_st", [P, 2, REP, TOK], F32R)
        k_st = sb("k_st", [P, 2, TOK], F32R)
        v_g = sb("v_g", [P, 2, TM, SD])
        mask = sb("mask", [P, P])
        e = sb("e", [P, 2, TM, TOK])
        e_t = sb("e_t", [P, TM, TOK])
        top = sb("top", [P, 2, TM])
        shift = sb("shift", [P, 2, TM])
        total = sb("total", [P, 2, TM])
        scale = sb("scale", [P, 2, TM])
        out_f = sb("out_f", [P, 2, TOK])
        score = [ctx.enter_context(nc.psum_tensor(f"s_score{i}", [P, TOK], F32)) for i in range(TM)]
        turn = [ctx.enter_context(nc.psum_tensor(f"s_turn{i}", [P, TOK], F32)) for i in range(2)]
        out = [ctx.enter_context(nc.psum_tensor(f"s_out{i}", [P, TOK], F32)) for i in range(2)]

        in_st = [sem(f"in_st{i}") for i in range(2)]
        mask_zero, mask_ready = sem("mask_zero"), sem("mask_ready")
        scored, top_ready, shift_ready, e_ready, scale_ready, norm_ready = (sem(n) for n in (
            "scored", "top_ready", "shift_ready", "e_ready", "scale_ready", "norm_ready"))
        turned, copied_a, copied_v, summed, out_copied, hi_ready, lo_ready = (sem(n) for n in (
            "turned", "copied_a", "copied_v", "summed", "out_copied", "hi_ready", "lo_ready"))
        G = 2 * REP
        ROUNDS = SH // G

        def load(sp, g, b):
            rows = keep["qk_dram"][bass.ds(g, 1), :, :, :].rearrange("o (j d) s n -> d (o j) s n", d=SD).bitcast(F32)
            for r in range(4):
                sp.dma_start(q_st[r * SD:(r + 1) * SD, b, :, :].bitcast(F32), rows[:, :, r % 2, :]).then_inc(in_st[b], 16)
            k_rows = keep["qk_dram"][QB:QB + KB, :, :, :].rearrange("c (j d) s n -> (c j) d s n", d=SD)[bass.ds(g, 1), :, :, :].rearrange("o d s n -> (o d) s n").bitcast(F32)
            for r in range(4):
                sp.dma_start(k_st[r * SD:(r + 1) * SD, b, :].bitcast(F32), k_rows[:, r // 2, :]).then_inc(in_st[b], 16)
            sp.dma_start(v_g[:, b, :, :], keep["v_dram"].rearrange("m p (g d) -> p m g d", d=SD)[:, :, bass.ds(g, 1), :].rearrange("p m o d -> p m (o d)")).then_inc(in_st[b], 16)

        def scores(pe, h, hl, first_tiles):
            b, j = hl // REP % 2, hl % REP
            for m in range(TM):
                if not first_tiles:
                    pe.wait_ge(e_ready, TM * h - TM + m + 1)
                nc.tensor.matmul(score[m][:, 0:TOK - m * P], q_st[:, b, j, m * P:(m + 1) * P], k_st[:, b, m * P:TOK], start=True, stop=True)
                nc.tensor.matmul(score[m][:, 0:P], keep["identity"][:], mask[:], start=False, stop=True, skip_group_check=True).then_inc(scored, 1)

        def turn_tile(pe, h, hl, r, kt):
            n = TM * h + r
            if r == 0:
                pe.wait_ge(norm_ready, TM * h + TM)
            for m in range(kt + 1):
                last = nc.tensor.transpose(turn[r % 2][:, m * P:(m + 1) * P], e[:, hl % 2, m, kt * P:(kt + 1) * P], keep["identity"][:])
            last.then_inc(turned, 1)

        def sum_tile(pe, h, hl, r, kt):
            b, j = hl // REP % 2, hl % REP
            if r < 2:
                pe.wait_ge(copied_a, 2 * h + r + 1)
            else:
                pe.wait_ge(copied_v, 2 * h + r - 1)
            nc.tensor.matmul(out[b][j * SD:(j + 1) * SD, 0:(kt + 1) * P], v_g[:, b, kt, :], e_t[:, kt, 0:(kt + 1) * P],
                             start=(r == 0), stop=(r == TM - 1), skip_group_check=True).then_inc(summed, 1)

        KTS = list(range(TM))[::-1]

        with nc.Block() as block:
            @block.sync
            def _(sp):
                load(sp, 0, 0)
                load(sp, 1, 1)
                with sp.Fori(1, ROUNDS) as r:
                    for b in range(2):
                        sp.wait_ge(summed, TM * G * r - (TM * REP if b == 0 else 0))
                        load(sp, 2 * r + b, b)

            @block.gpsimd
            def _(pool):
                nc.gpsimd.memset(mask[:], 0.0).then_inc(mask_zero, 1)
                pool.wait_ge(mask_zero, 1)
                nc.gpsimd.affine_select(out=mask[:], in_=mask[:], compare_op=ALU.is_ge, fill=MASKED, base=0,
                                        pattern=[[1, P]], channel_multiplier=-1).then_inc(mask_ready, 1)

            def act_exps(act, h, hl):
                b = hl % 2
                act.wait_ge(shift_ready, h + 1)
                for m in range(TM):
                    nc.scalar.activation(e[:, b, m, m * P:TOK], score[m][:, 0:TOK - m * P], ACT.Exp, bias=shift[:, b, m:m + 1], scale=SSCALE,
                                         accum_out=total[:, b, m:m + 1]).then_inc(e_ready, 1)

            def act_copies(act, h, first):
                for r in range(2):
                    act.wait_ge(turned, TM * h + r + 1)
                    if not first:
                        act.wait_ge(summed, TM * h - TM + r + 1)
                    kt = KTS[r]
                    nc.scalar.activation(e_t[:, kt, 0:(kt + 1) * P], turn[r % 2][:, 0:(kt + 1) * P], ACT.Copy).then_inc(copied_a, 1)

            def act_out(act, g, b):
                act.wait_ge(summed, TM * REP * g + TM * REP)
                act.wait_ge(lo_ready, g + 1)
                nc.scalar.activation(out_f[:, b, :], out[b][:], ACT.Copy).then_inc(out_copied, 1)

            @block.scalar
            def _(act):
                act_exps(act, 0, 0)

                def body(r, first=False, last=False):
                    for hl in range(G):
                        h = G * r + hl
                        act_copies(act, h, first and hl == 0)
                        if hl % REP == 0 and not (first and hl == 0):
                            act_out(act, 2 * r + hl // REP - 1, 1 - hl // REP)
                        if not (last and hl == G - 1):
                            act_exps(act, h + 1, hl + 1)
                body(0, first=True)
                with act.Fori(1, ROUNDS - 1) as r:
                    body(r)
                body(ROUNDS - 1, last=True)
                act_out(act, SKV - 1, 1)

            def dve_tops(dve, h, hl):
                b = hl % 2
                for m in range(TM):
                    dve.wait_ge(scored, TM * h + m + 1)
                    nc.vector.tensor_reduce(top[:, b, m:m + 1], score[m][:, 0:TOK - m * P], AX.X, ALU.max).then_inc(top_ready, 1)
                dve.wait_ge(top_ready, TM * h + TM)
                nc.vector.tensor_scalar(shift[:, b, :], top[:, b, :], -SSCALE, None, ALU.mult).then_inc(shift_ready, 1)

            def dve_norms(dve, h, hl):
                b = hl % 2
                dve.wait_ge(e_ready, TM * h + TM)
                nc.vector.reciprocal(scale[:, b, :], total[:, b, :]).then_inc(scale_ready, 1)
                dve.wait_ge(scale_ready, h + 1)
                for m in range(TM):
                    nc.vector.tensor_scalar(e[:, b, m, m * P:TOK], e[:, b, m, m * P:TOK], scale[:, b, m:m + 1], None, ALU.mult).then_inc(norm_ready, 1)

            def dve_copies(dve, h, first):
                for r in range(2, TM):
                    dve.wait_ge(turned, TM * h + r + 1)
                    if not first:
                        dve.wait_ge(summed, TM * h - TM + r + 1)
                    kt = KTS[r]
                    nc.vector.tensor_copy(e_t[:, kt, 0:(kt + 1) * P], turn[r % 2][:, 0:(kt + 1) * P]).then_inc(copied_v, 1)

            def dve_split(dve, g, b):
                dve.wait_ge(out_copied, g + 1)
                hi = keep["a_hi"][:, bass.ds(g, 1), :].rearrange("p o n -> p (o n)")
                lo = keep["a_lo"][:, bass.ds(g, 1), :].rearrange("p o n -> p (o n)")
                nc.vector.tensor_scalar(hi, out_f[:, b, :], 1.0, None, ALU.mult).then_inc(hi_ready, 1)
                dve.wait_ge(hi_ready, g + 1)
                nc.vector.tensor_tensor(lo, out_f[:, b, :], hi.bitcast(F32), ALU.subtract).then_inc(lo_ready, 1)

            @block.vector
            def _(dve):
                dve.sem_inc(lo_ready, 2)
                dve_tops(dve, 0, 0)

                def body(r, first=False, last=False):
                    for hl in range(G):
                        h = G * r + hl
                        dve_norms(dve, h, hl)
                        if not (last and hl == G - 1):
                            dve_tops(dve, h + 1, hl + 1)
                        dve_copies(dve, h, first and hl == 0)
                        if hl % REP == 1 and not (first and hl == 1):
                            dve_split(dve, 2 * r + hl // REP - 1, 1 - hl // REP)
                body(0, first=True)
                with dve.Fori(1, ROUNDS - 1) as r:
                    body(r)
                body(ROUNDS - 1, last=True)
                dve_split(dve, SKV - 1, 1)

            @block.tensor
            def _(pe):
                pe.wait_ge(mask_ready, 1)
                pe.wait_ge(in_st[0], 144)
                scores(pe, 0, 0, True)

                def body(r, first=False, last=False):
                    for hl in range(G):
                        h = G * r + hl
                        if not (last and hl == G - 1):
                            if hl == REP - 1:
                                pe.wait_ge(in_st[1], 144 * r + 144)
                            if hl == G - 1:
                                pe.wait_ge(in_st[0], 144 * r + 288)
                            scores(pe, h + 1, (hl + 1) % G, False)
                        turn_tile(pe, h, hl, 0, KTS[0])
                        turn_tile(pe, h, hl, 1, KTS[1])
                        if hl % REP == 0 and not first:
                            pe.wait_ge(out_copied, 2 * r + hl // REP - 1)
                        sum_tile(pe, h, hl, 0, KTS[0])
                        pe.wait_ge(copied_a, 2 * h + 1)
                        turn_tile(pe, h, hl, 2, KTS[2])
                        sum_tile(pe, h, hl, 1, KTS[1])
                        turn_tile(pe, h, hl, 3, KTS[3])
                        sum_tile(pe, h, hl, 2, KTS[2])
                        sum_tile(pe, h, hl, 3, KTS[3])

                body(0, first=True)
                with pe.Fori(1, ROUNDS - 1) as r:
                    body(r)
                body(ROUNDS - 1, last=True)


E = 16
TOP = 4
I = 384
IK = I // P
GU = 2 * P


def route(nc, io, keep):
    with ExitStack() as ctx:
        def sb(n, shape, dt=F32):
            return ctx.enter_context(nc.sbuf_tensor("r_" + n, shape, dt))

        def sem(n):
            return nc.alloc_semaphore("r_" + n)

        w_raw = sb("w_raw", [P, DK, E])
        w_hi = sb("w_hi", [P, DK, E], F32R)
        w_lo = sb("w_lo", [P, DK, E], F32R)
        e_bias = sb("e_bias", [P, E])
        logit_t = sb("logit_t", [E, TOK])
        prob = sb("prob", [P, TM, E])
        left = sb("left", [P, TM, E])
        first = sb("first", [P, TM, E])
        chosen = sb("chosen", [P, TM, E])
        rank = sb("rank", [P, TM, E])
        best = sb("best", [P, TM])
        logits = ctx.enter_context(nc.psum_tensor("r_logits", [P, TOK], F32))
        turned = ctx.enter_context(nc.psum_tensor("r_turned", [P, TM * E], F32))
        in_w, rank_ready, w_hi_ready, w_lo_ready, banked, copied, turned_ready, prob_ready, v_chain = (sem(n) for n in (
            "in_w", "rank_ready", "w_hi_ready", "w_lo_ready", "banked", "copied", "turned_ready", "prob_ready", "v_chain"))

        with nc.Block() as block:
            @block.sync
            def _(sp):
                sp.dma_start(w_raw[:], io["router_t"]).then_inc(in_w, 16)
                sp.dma_start(e_bias[:], broadcast_rows(io["e_bias"], P)).then_inc(in_w, 16)

            @block.gpsimd
            def _(pool):
                for n in range(E):
                    last = nc.gpsimd.memset(rank[:, :, n:n + 1], float(E - n))
                    last.then_inc(rank_ready, 1)

            @block.scalar
            def _(act):
                act.wait_ge(in_w, 32)
                nc.scalar.activation(w_hi[:], w_raw[:], ACT.Copy).then_inc(w_hi_ready, 1)
                act.wait_ge(banked, 1)
                nc.scalar.activation(logit_t[:], logits[0:E, :], ACT.Copy).then_inc(copied, 1)
                act.wait_ge(turned_ready, 1)
                nc.scalar.activation(prob[:], turned[:, :].rearrange("p (m e) -> p m e", e=E), ACT.Sigmoid).then_inc(prob_ready, 1)

            @block.tensor
            def _(pe):
                pe.wait_ge(w_lo_ready, 1)
                for k in range(DK):
                    for a, (w, x) in enumerate([(w_hi, "xt_hi"), (w_lo, "xt_hi"), (w_hi, "xt_lo")]):
                        last = nc.tensor.matmul(logits[0:E, :], w[:, k, :], keep[x][:, k, :], start=(k == 0 and a == 0), stop=(k == DK - 1 and a == 2))
                last.then_inc(banked, 1)
                pe.wait_ge(copied, 1)
                for m in range(TM):
                    last = nc.tensor.transpose(turned[:, m * E:(m + 1) * E], logit_t[:, m * P:(m + 1) * P], keep["identity"][0:E, 0:E])
                last.then_inc(turned_ready, 1)

            @block.vector
            def _(dve):
                links = [0]

                def link(ins):
                    links[0] += 1
                    ins.then_inc(v_chain, 1)
                    dve.wait_ge(v_chain, links[0])

                dve.wait_ge(w_hi_ready, 1)
                nc.vector.tensor_tensor(w_lo[:], w_raw[:], w_hi[:].bitcast(F32), ALU.subtract).then_inc(w_lo_ready, 1)
                link(nc.vector.memset(chosen[:], 0.0))
                dve.wait_ge(rank_ready, E)
                dve.wait_ge(prob_ready, 1)
                by_token = lambda t: t[:, :].rearrange("p (m o) -> p m o", o=1).broadcast_to([P, TM, E])
                link(nc.vector.tensor_tensor(left[:], prob[:], e_bias[:, :].rearrange("p (o e) -> p o e", o=1).broadcast_to([P, TM, E]), ALU.add))
                for _ in range(TOP):
                    link(nc.vector.tensor_reduce(best[:], left[:], AX.X, ALU.max))
                    link(nc.vector.tensor_tensor(first[:], left[:], by_token(best), ALU.is_equal))
                    link(nc.vector.tensor_tensor(first[:], first[:], rank[:], ALU.mult))
                    link(nc.vector.tensor_reduce(best[:], first[:], AX.X, ALU.max))
                    link(nc.vector.tensor_tensor(first[:], first[:], by_token(best), ALU.is_equal))
                    link(nc.vector.tensor_tensor(chosen[:], chosen[:], first[:], ALU.add))
                    link(nc.vector.tensor_scalar(first[:], first[:], -3.0e38, None, ALU.mult))
                    link(nc.vector.tensor_tensor(left[:], left[:], first[:], ALU.add))
                link(nc.vector.tensor_tensor(prob[:], prob[:], chosen[:], ALU.mult))
                link(nc.vector.tensor_reduce(best[:], prob[:], AX.X, ALU.add))
                link(nc.vector.tensor_scalar(best[:], best[:], 1e-20, None, ALU.add))
                link(nc.vector.reciprocal(best[:], best[:]))
                link(nc.vector.memset(keep["combine"][:], 1.0))
                link(nc.vector.tensor_tensor(keep["combine"][:, :, 0:E], prob[:], by_token(best), ALU.mult))


def experts(nc, io, keep):
    with ExitStack() as ctx:
        def sb(n, shape, dt=F32):
            return ctx.enter_context(nc.sbuf_tensor("f_" + n, shape, dt))

        def sem(n):
            return nc.alloc_semaphore("f_" + n)

        gu_raw = [sb(f"gu_raw{i}", [P, DK, GU]) for i in range(IK)]
        gu_hi = [sb(f"gu_hi{i}", [P, DK, GU], F32R) for i in range(IK)]
        gu_lo = [sb(f"gu_lo{i}", [P, DK, GU], F32R) for i in range(IK)]
        dn_raw = sb("dn_raw", [P, IK, D])
        dn_hi = sb("dn_hi", [P, IK, D], F32R)
        dn_lo = sb("dn_lo", [P, IK, D], F32R)
        silu = sb("silu", [P, IK, TOK])
        h_f = sb("h_f", [P, IK, TOK])
        h_hi = sb("h_hi", [P, IK, TOK], F32R)
        h_lo = sb("h_lo", [P, IK, TOK], F32R)
        weight = sb("weight", [P, TM])
        gate = [ctx.enter_context(nc.psum_tensor(f"f_gate{i}", [P, TOK], F32)) for i in range(2)]
        up = [ctx.enter_context(nc.psum_tensor(f"f_up{i}", [P, TOK], F32)) for i in range(2)]
        y = [ctx.enter_context(nc.psum_tensor(f"f_y{i}", [P, 512], F32)) for i in range(4)]

        in_gu = [sem(f"in_gu{i}") for i in range(IK)]
        hi_gu = [sem(f"hi_gu{i}") for i in range(IK)]
        lo_gu = [sem(f"lo_gu{i}") for i in range(IK)]
        used_gu = [sem(f"used_gu{i}") for i in range(IK)]
        in_dn, hi_dn, lo_dn = sem("in_dn"), sem("hi_dn"), sem("lo_dn")
        silu_ready, h_ready, h_hi_ready, h_lo_ready = sem("silu_ready"), sem("h_ready"), sem("h_hi_ready"), sem("h_lo_ready")
        weight_ready, y_banked, y_taken, stored = sem("weight_ready"), sem("y_banked"), sem("y_taken"), sem("stored")
        x = keep["x"]
        N = E + 1
        Y = 2 * TM

        with nc.Block() as block:
            @block.sync
            def _(sp):
                def load_gu(e, i):
                    src = io["gate_up"][bass.ds(e, 1), i, :, :, :].rearrange("o p k n -> p (o k) n")
                    sp.dma_start(gu_raw[i][:], src).then_inc(in_gu[i], 16)

                def load_dn(e):
                    sp.dma_start(dn_raw[:], io["down"][bass.ds(e, 1), :, :, :].rearrange("o p k n -> p (o k) n")).then_inc(in_dn, 16)

                for i in range(IK):
                    load_gu(0, i)
                load_dn(0)
                with sp.Fori(1, N) as e:
                    for i in range(IK):
                        sp.wait_ge(lo_gu[i], e)
                        load_gu(e, i)
                    sp.wait_ge(lo_dn, e)
                    load_dn(e)
                for m in range(TM):
                    sp.wait_ge(y_taken, 4 + Y * (N - 1) + 2 * m + 2)
                    sp.dma_start(io["out"][0, m * P:(m + 1) * P, :], x[:, m, :]).then_inc(stored, 16)
                sp.wait_ge(stored, 16 * TM)

            @block.scalar
            def _(act):
                def split_gu(e, i):
                    act.wait_ge(in_gu[i], 16 * e + 16)
                    nc.scalar.activation(gu_hi[i][:], gu_raw[i][:], ACT.Copy).then_inc(hi_gu[i], 1)

                def split_dn(e):
                    act.wait_ge(in_dn, 16 * e + 16)
                    nc.scalar.activation(dn_hi[:], dn_raw[:], ACT.Copy).then_inc(hi_dn, 1)

                def body(e, more):
                    for i in range(IK):
                        act.wait_ge(used_gu[i], e + 1)
                        nc.scalar.activation(silu[:, i, :], gate[i % 2][:], ACT.Silu).then_inc(silu_ready, 1)
                        act.wait_ge(h_ready, 3 * e + i + 2)
                        nc.scalar.activation(h_hi[:, i, :], h_f[:, i, :], ACT.Copy).then_inc(h_hi_ready, 1)
                        if more:
                            split_gu(e + 1, i)
                    if more:
                        act.wait_ge(y_banked, Y * e + Y)
                        split_dn(e + 1)

                for i in range(IK):
                    split_gu(0, i)
                split_dn(0)
                with act.Fori(0, N - 1) as e:
                    body(e, True)
                body(N - 1, False)

            @block.vector
            def _(dve):
                def split_gu(e, i):
                    dve.wait_ge(hi_gu[i], e + 1)
                    nc.vector.tensor_tensor(gu_lo[i][:], gu_raw[i][:], gu_hi[i][:].bitcast(F32), ALU.subtract).then_inc(lo_gu[i], 1)

                def split_dn(e):
                    dve.wait_ge(hi_dn, e + 1)
                    nc.vector.tensor_tensor(dn_lo[:], dn_raw[:], dn_hi[:].bitcast(F32), ALU.subtract).then_inc(lo_dn, 1)

                def body(e, more):
                    dve.wait_ge(y_taken, 4 + Y * e)
                    nc.vector.tensor_scalar(weight[:], keep["combine"][:, :, bass.ds(e, 1)].rearrange("p m o -> p (m o)"), 1.0, None, ALU.mult).then_inc(weight_ready, 1)
                    for i in range(IK):
                        dve.wait_ge(silu_ready, 3 * e + i + 1)
                        nc.vector.tensor_tensor(h_f[:, i, :], up[i % 2][:], silu[:, i, :], ALU.mult).then_inc(h_ready, 1)
                        dve.wait_ge(h_hi_ready, 3 * e + i + 1)
                        nc.vector.tensor_tensor(h_lo[:, i, :], h_f[:, i, :], h_hi[:, i, :].bitcast(F32), ALU.subtract).then_inc(h_lo_ready, 1)
                        if more:
                            split_gu(e + 1, i)
                    dve.wait_ge(weight_ready, e + 1)
                    for n in range(Y):
                        m, half = divmod(n, 2)
                        cols = slice(half * 512, (half + 1) * 512)
                        dve.wait_ge(y_banked, Y * e + n + 1)
                        nc.vector.scalar_tensor_tensor(out=x[:, m, cols], in0=y[n % 4][:], scalar=weight[:, m:m + 1], in1=x[:, m, cols],
                                                       op0=ALU.mult, op1=ALU.add).then_inc(y_taken, 1)
                    if more:
                        split_dn(e + 1)

                dve.sem_inc(h_ready, 1)
                dve.sem_inc(y_taken, 4)
                for i in range(IK):
                    split_gu(0, i)
                split_dn(0)
                with dve.Fori(0, N - 1) as e:
                    body(e, True)
                body(N - 1, False)

            @block.tensor
            def _(pe):
                def gate_up(e, i):
                    pe.wait_ge(lo_gu[i], e + 1)
                    if i != 1:
                        pe.wait_ge(h_ready, 3 * e + (1 if i == 0 else 2))
                    for bank, c in ((gate[i % 2], 0), (up[i % 2], P)):
                        for k in range(DK):
                            for a, (w, xt) in enumerate([(gu_hi, "xt_hi"), (gu_lo, "xt_hi"), (gu_hi, "xt_lo")]):
                                last = nc.tensor.matmul(bank[:], w[i][:, k, c:c + P], keep[xt][:, k, :], start=(k == 0 and a == 0), stop=(k == DK - 1 and a == 2))
                    last.then_inc(used_gu[i], 1)

                def down(e, n, i):
                    m, half = divmod(n, 2)
                    for a, (h, w) in enumerate([(h_hi, dn_hi), (h_hi, dn_lo), (h_lo, dn_hi)]):
                        last = nc.tensor.matmul(y[n % 4][:], h[:, i, m * P:(m + 1) * P], w[:, i, half * 512:(half + 1) * 512],
                                                start=(i == 0 and a == 0), stop=(i == IK - 1 and a == 2))
                    if i == IK - 1:
                        last.then_inc(y_banked, 1)
                    return last

                def body(e):
                    for i in range(IK):
                        gate_up(e, i)
                    pe.wait_ge(lo_dn, e + 1)
                    pe.wait_ge(h_lo_ready, 3 * e + 2)
                    for n in range(4):
                        pe.wait_ge(y_taken, Y * e + n + 1)
                        for i in range(IK - 1):
                            down(e, n, i)
                    pe.wait_ge(h_lo_ready, 3 * e + 3)
                    for n in range(4):
                        down(e, n, IK - 1)
                    for n in range(4, Y):
                        pe.wait_ge(y_taken, Y * e + n + 1)
                        for i in range(IK):
                            down(e, n, i)

                with pe.Fori(0, N) as e:
                    body(e)


def build(nc, io):
    with ExitStack() as ctx:
        def sb(name, shape, dt=F32):
            return ctx.enter_context(nc.sbuf_tensor(name, shape, dt))

        keep = {
            "identity": sb("identity", [P, P]),
            "bias_k": sb("bias_k", [P, PAIRS + 1]),
            "bias_v": sb("bias_v", [P, PAIRS + 1]),
            "guard": sb("guard", [P, XH + 2, 2]),
            "q_dram": nc.dram_tensor("q_scratch", [PAIRS + 1, P, 2, TOK], F32R).ap(),
            "dca_dram": nc.dram_tensor("dca_scratch", [P, PAIRS, TOK], F32).ap(),
            "o_dram": nc.dram_tensor("o_scratch", [PAIRS, P, TOK], F32).ap(),
            "sum_dram": nc.dram_tensor("sum_scratch", [XH, TOK], F32).ap(),
            "qk_dram": nc.dram_tensor("qk_scratch", [QB + KB, P, 2, TOK], F32R).ap(),
            "v_dram": nc.dram_tensor("v_scratch", [TM, P, SKV * SD], F32).ap(),
        }
        with nc.cleanup_on_exit(), ExitStack() as inner:
            keep["q_t"] = inner.enter_context(nc.sbuf_tensor("q_t", [P, PAIRS, TOK], F32))
            prepare(nc, io, keep)
            second_attention(nc, io, keep)
        with nc.cleanup_on_exit():
            cross_attention(nc, io, keep)

        keep["x"] = sb("x_now", [P, TM, D])
        keep["xt_hi"] = sb("xt_hi", [P, DK, TOK], F32R)
        keep["xt_lo"] = sb("xt_lo", [P, DK, TOK], F32R)
        with nc.cleanup_on_exit(), ExitStack() as inner:
            keep["a_hi"] = inner.enter_context(nc.sbuf_tensor("a_hi", [P, DK, TOK], F32R))
            keep["a_lo"] = inner.enter_context(nc.sbuf_tensor("a_lo", [P, DK, TOK], F32R))
            combine_attentions(nc, io, keep)
            project_and_norm(nc, "xo", io["wo_cross"], io["bo"], io["x"][0], keep)
            project_qkv(nc, io, keep)
            self_attention(nc, io, keep)
            project_and_norm(nc, "so", io["wo_self"], None, None, keep)
        keep["combine"] = sb("combine", [P, TM, E + 1])
        route(nc, io, keep)
        experts(nc, io, keep)


def kernel(**inputs):
    import numpy as np
    import concourse.bacc as bacc
    from concourse.bass_utils import run_bass_kernel_spmd

    cross = {n[len("L0_xattn_"):]: np.asarray(a) for n, a in inputs.items() if n.startswith("L0_xattn_")}
    own = {n[len("L0_attn_"):]: np.asarray(a) for n, a in inputs.items() if n.startswith("L0_attn_")}
    ffn = {n[len("L0_ffn_"):]: np.asarray(a) for n, a in inputs.items() if n.startswith("L0_ffn_")}
    context = np.asarray(inputs["ctx_1024"])[0]

    def by_pair(w):
        return w.reshape(CK, P, PAIRS, P).transpose(2, 1, 0, 3)

    heads = np.concatenate([cross["Wk"], cross["Wv"]], 1).reshape(KC, XH, 2, XD)
    head_bias = np.concatenate([cross["bk"], cross["bv"]]).reshape(XH, 2, XD)
    wkv = np.stack([by_pair(heads[:, :, s, :].reshape(KC, D)) for s in range(2)], 2)
    gate_up = np.concatenate([ffn["gate_up_proj"], np.concatenate([ffn["shared_gate_w"], ffn["shared_up_w"]], 0)[None]], 0)
    down = np.concatenate([ffn["down_proj"], ffn["shared_down_w"][None]], 0)
    data = {
        "x": np.asarray(inputs["x"]),
        "ctx_t": context.T.reshape(CK, P, STEPS, CHUNK).transpose(2, 1, 0, 3),
        "dca_t": context[CTX - DCA:].T.reshape(CK, P, DCA).transpose(1, 0, 2),
        "wq": cross["Wq"], "bq": cross["bq"], "qn_w": cross["qn_w"], "qn_b": cross["qn_b"], "kn_w": cross["kn_w"],
        "bk": head_bias[:, 0].reshape(PAIRS, P).T, "bv": head_bias[:, 1].reshape(PAIRS, P).T,
        "wkv": np.concatenate([wkv, wkv[:1]], 0),
        "wkv_dca": cross["Wkv_dca"], "bkv_dca": cross["bkv_dca"], "kn_dca_w": cross["kn_dca_w"], "kn_dca_b": cross["kn_dca_b"],
        "wo_cross": cross["Wo"], "bo": cross["bo"],
        "wqk": np.concatenate([own["wq"], own["wk"]], 1).reshape(DK, P, QB + KB, P).transpose(2, 1, 0, 3),
        "wv": own["wv"], "wo_self": own["wo"],
        "router_t": ffn["router_w"].T.reshape(DK, P, E).transpose(1, 0, 2), "e_bias": ffn["e_bias"],
        "gate_up": gate_up.reshape(E + 1, 2, IK, P, DK, P).transpose(0, 2, 5, 4, 1, 3).reshape(E + 1, IK, P, DK, GU),
        "down": down.transpose(0, 2, 1).reshape(E + 1, IK, P, D).transpose(0, 2, 1, 3),
    }
    nc = bacc.Bacc("TRN2", target_bir_lowering=False, num_devices=1)
    arrays, io = {}, {}
    for name, a in data.items():
        a = np.ascontiguousarray(a)
        arrays[f"in_{name}_dram"] = a
        io[name] = nc.dram_tensor(f"in_{name}_dram", a.shape, mybir.dt.from_np(a.dtype), kind="ExternalInput").ap()
    io["out"] = nc.dram_tensor("out_dram", (1, TOK, D), F32, kind="ExternalOutput").ap()
    build(nc, io)
    result = run_bass_kernel_spmd(nc, [arrays], core_ids=[0])
    return result.results[0]["out_dram"]
```
